# Optimizing a Trainium2 kernel written in Bass

```python
import numpy as np
import jax
import jax.numpy as jnp

def _softmax(x, axis=-1):
    return jax.nn.softmax(x, axis=axis)

def _gelu(x):
    return jax.nn.gelu(x, approximate=True)

def _silu(x):
    return jax.nn.silu(x)

def _sigmoid(x):
    return jax.nn.sigmoid(x)

def _layernorm(x, axis=-1, eps=1e-05):
    m = jnp.mean(x, axis=axis, keepdims=True)
    v = jnp.var(x, axis=axis, keepdims=True)
    return (x - m) / jnp.sqrt(v + eps)

def _scatter_add(tgt, idx, src, axis=0):
    return tgt.at[idx].add(src)

def _segment_sum(src, seg, n):
    return jax.ops.segment_sum(src, seg, n)
kernel_name = 'mk_xattn_ffn_d1_seqx_r2_da9967'

def setup_inputs(seed: int=0):
    np.random.seed(seed)
    _w = jnp.asarray

    def _rec_inputs():
        import jax
        import jax.numpy as jnp
        _rk = jax.random.key(seed)
        x = 0.0002279 + 0.9999 * jax.random.normal(jax.random.fold_in(_rk, 1), (16, 1024, 512), jnp.float32)
        _lenS = 1024 - jax.random.randint(jax.random.fold_in(_rk, 7), (16,), 0, max(1, 1024 // 4) + 1, jnp.int32)
        _lenS2 = 64 - jax.random.randint(jax.random.fold_in(_rk, 8), (16,), 0, max(1, 64 // 4) + 1, jnp.int32)
        _ctx_1024P = jax.random.normal(jax.random.fold_in(_rk, 11), (16, 16, 512), jnp.float32)
        _ctx_1024c = jax.random.dirichlet(jax.random.fold_in(_rk, 511), 0.3 * jnp.ones((16,), jnp.float32), (16, 64))
        _ctx_1024t = jnp.einsum('bsk,bkd->bsd', _ctx_1024c, _ctx_1024P)
        _ctx_1024t = _ctx_1024t * jax.lax.rsqrt(jnp.mean(jnp.square(_ctx_1024t)) + 1e-12) * 0.953939
        ctx_1024 = -0.000392918 + 0.999932 * (_ctx_1024t + 0.3 * jax.random.normal(jax.random.fold_in(_rk, 611), (16, 64, 512), jnp.float32))
        fside_Bx16_0 = 0.119436 + 0.907674 * jax.random.normal(jax.random.fold_in(_rk, 12), (16, 16), jnp.float32)
        return (x, ctx_1024, fside_Bx16_0)
    x, ctx_1024, fside_Bx16_0 = _rec_inputs()

    def _L0_xattn_setup():
        import jax, jax.numpy as jnp
        import numpy as np
        DIM = 512
        HEADS = 16
        DIM_HEAD = 64
        INNER = HEADS * DIM_HEAD
        EPS = 1e-05

        def layernorm(x, w, b):
            mu = jnp.mean(x, axis=-1, keepdims=True)
            var = jnp.mean(jnp.square(x - mu), axis=-1, keepdims=True)
            return (x - mu) * jax.lax.rsqrt(var + EPS) * w + b
        key = jax.random.key(seed)
        ks = jax.random.split(key, 9)
        b, n1, n2 = (4, 2048, 128)
        x = jax.random.normal(ks[0], (b, n1, DIM), dtype=jnp.float32)
        latents = jax.random.normal(ks[1], (b, n2, DIM), dtype=jnp.float32)
        shift = jax.random.normal(ks[2], (b, HEADS), dtype=jnp.float32)
        scale = jax.random.normal(ks[3], (b, HEADS), dtype=jnp.float32)
        s = 1.0 / np.sqrt(DIM)
        Wq = jax.random.normal(ks[4], (DIM, INNER), dtype=jnp.float32) * s
        Wkv = jax.random.normal(ks[5], (DIM, 2 * INNER), dtype=jnp.float32) * s
        Wout = jax.random.normal(ks[6], (INNER, DIM), dtype=jnp.float32) * (1.0 / np.sqrt(INNER))
        ln1_w = jnp.ones((DIM,), jnp.float32)
        ln1_b = jnp.zeros((DIM,), jnp.float32)
        ln2_w = jnp.ones((DIM,), jnp.float32)
        ln2_b = jnp.zeros((DIM,), jnp.float32)
        return {'x': x, 'latents': latents, 'shift': shift, 'scale': scale, 'ln1_w': ln1_w, 'ln1_b': ln1_b, 'ln2_w': ln2_w, 'ln2_b': ln2_b, 'Wq': Wq, 'Wkv': Wkv, 'Wout': Wout}
    _L0_xattn_all = _L0_xattn_setup()
    _L0_xattn_in = {k: v for k, v in _L0_xattn_all.items() if k in ('ln1_w', 'ln1_b', 'ln2_w', 'ln2_b', 'Wq', 'Wkv', 'Wout')}
    del _L0_xattn_all

    def _L0_ffn_setup():
        import jax, jax.numpy as jnp
        import numpy as np
        D_MODEL = 512
        key = jax.random.key(seed)
        k_x, k_w, k_a1, k_a2 = jax.random.split(key, 4)
        x = jax.random.normal(k_x, (4, 1024, D_MODEL), dtype=jnp.float32)
        weight = jax.random.normal(k_w, (D_MODEL, D_MODEL), dtype=jnp.float32) * 0.02
        aux_weight1 = jax.random.normal(k_a1, (D_MODEL, D_MODEL), dtype=jnp.float32) * 0.02
        aux_weight2 = jax.random.normal(k_a2, (D_MODEL, D_MODEL), dtype=jnp.float32) * 0.02
        bias = jnp.zeros((D_MODEL,), dtype=jnp.float32)
        return {'x': x, 'weight': weight, 'aux_weight1': aux_weight1, 'aux_weight2': aux_weight2, 'bias': bias}
    _L0_ffn_all = _L0_ffn_setup()
    _L0_ffn_in = {k: v for k, v in _L0_ffn_all.items() if k in ('weight', 'aux_weight1', 'aux_weight2', 'bias')}
    del _L0_ffn_all
    return {'x': x, 'ctx_1024': ctx_1024, 'fside_Bx16_0': fside_Bx16_0, 'L0_xattn_ln1_w': _L0_xattn_in['ln1_w'], 'L0_xattn_ln1_b': _L0_xattn_in['ln1_b'], 'L0_xattn_ln2_w': _L0_xattn_in['ln2_w'], 'L0_xattn_ln2_b': _L0_xattn_in['ln2_b'], 'L0_xattn_Wq': _L0_xattn_in['Wq'], 'L0_xattn_Wkv': _L0_xattn_in['Wkv'], 'L0_xattn_Wout': _L0_xattn_in['Wout'], 'L0_ffn_weight': _L0_ffn_in['weight'], 'L0_ffn_aux_weight1': _L0_ffn_in['aux_weight1'], 'L0_ffn_aux_weight2': _L0_ffn_in['aux_weight2'], 'L0_ffn_bias': _L0_ffn_in['bias']}

def reference(x, ctx_1024, fside_Bx16_0, L0_xattn_ln1_w, L0_xattn_ln1_b, L0_xattn_ln2_w, L0_xattn_ln2_b, L0_xattn_Wq, L0_xattn_Wkv, L0_xattn_Wout, L0_ffn_weight, L0_ffn_aux_weight1, L0_ffn_aux_weight2, L0_ffn_bias):
    import jax
    import jax.numpy as jnp

    def _L0_xattn_ref(x, latents, shift, scale, ln1_w, ln1_b, ln2_w, ln2_b, Wq, Wkv, Wout):
        import jax, jax.numpy as jnp
        import numpy as np
        DIM = 512
        HEADS = 16
        DIM_HEAD = 64
        INNER = HEADS * DIM_HEAD
        EPS = 1e-05

        def layernorm(x, w, b):
            mu = jnp.mean(x, axis=-1, keepdims=True)
            var = jnp.mean(jnp.square(x - mu), axis=-1, keepdims=True)
            return (x - mu) * jax.lax.rsqrt(var + EPS) * w + b
        b = x.shape[0]
        xn = layernorm(x, ln1_w, ln1_b)
        ln = layernorm(latents, ln2_w, ln2_b)
        q = ln @ Wq
        kv = xn @ Wkv
        k, v = jnp.split(kv, 2, axis=-1)
        q = q.reshape(b, -1, HEADS, DIM_HEAD)
        k = k.reshape(b, -1, HEADS, DIM_HEAD)
        v = v.reshape(b, -1, HEADS, DIM_HEAD)
        q = q * (1.0 + scale[:, None, :, None]) + shift[:, None, :, None]
        attn_scale = DIM_HEAD ** (-0.5)
        qk = jnp.einsum('bihd,bjhd->bhij', q.astype(jnp.float32), k.astype(jnp.float32)) * attn_scale
        attn = jax.nn.softmax(qk, axis=-1).astype(v.dtype)
        out = jnp.einsum('bhij,bjhd->bihd', attn, v)
        out = out.reshape(b, -1, INNER)
        return out @ Wout

    def _L0_ffn_ref(x, weight, aux_weight1, aux_weight2, bias):
        import jax, jax.numpy as jnp
        import numpy as np
        D_MODEL = 512
        h = jnp.einsum('btc,cd->btd', x, weight)
        h = jnp.einsum('btc,cd->btd', h, aux_weight1)
        h = jnp.einsum('btc,cd->btd', h, aux_weight2)
        return jnp.tanh(h + bias)
    x = x + _L0_xattn_ref(ctx_1024, _layernorm(x, axis=-1), fside_Bx16_0, fside_Bx16_0, L0_xattn_ln1_w, L0_xattn_ln1_b, L0_xattn_ln2_w, L0_xattn_ln2_b, L0_xattn_Wq, L0_xattn_Wkv, L0_xattn_Wout)
    x = x + _L0_ffn_ref(_layernorm(x, axis=-1), L0_ffn_weight, L0_ffn_aux_weight1, L0_ffn_aux_weight2, L0_ffn_bias)
    return x

_drawn_inputs = setup_inputs


def setup_inputs(seed=0):
    import zlib

    import numpy as np

    out = dict(_drawn_inputs(seed))
    spreads = {'L0_xattn_ln1_w': (1.0, 0.2),
     'L0_xattn_ln1_b': (0.0, 0.1),
     'L0_xattn_ln2_w': (1.0, 0.2),
     'L0_xattn_ln2_b': (0.0, 0.1),
     'L0_ffn_bias': (0.0, 0.1)}
    factors = {}
    for name, (base, spread) in spreads.items():
        noise = np.random.default_rng([zlib.crc32(name.encode()), seed]).standard_normal(out[name].shape)
        drawn = base * np.exp(spread * noise) if base else spread * noise
        out[name] = jnp.asarray(drawn.astype(out[name].dtype))
    for name, factor in factors.items():
        out[name] = (out[name] * factor).astype(out[name].dtype)
    return out
```

```python
from contextlib import ExitStack

import numpy as np

import concourse.bass as bass
from concourse import mybir

F32 = mybir.dt.float32
F32R = mybir.dt.float32r
ALU = mybir.AluOpType
ACT = mybir.ActivationFunctionType
AX_X = mybir.AxisListType.X

P = 128
BANK = 512
EPS = 1e-5
B, ROWS, D = 16, 1024, 512
CTX, H, DH = 64, 16, 64
INNER = H * DH
PAIRS = H // 2
DC = D // P
TPB = ROWS // P
T = B * TPB
RING = 4
SCALE = DH ** -0.5
assert DH == CTX == P // 2 and D == BANK and INNER == 2 * BANK and TPB == 8 and TPB % RING == 0


def build(nc, x, ctx_rows, fs_cols, ln1_w, ln1_b, ln2_w, ln2_b, wqT, wkv, wout, ffn_wT, aux1T, aux2,
          ffn_bias, ident_in, out):
    kv_scratch = nc.dram_tensor("kv_scratch", (2, PAIRS, P, B, CTX), F32, kind="Internal").ap()
    x_t = x.rearrange("b (n p) d -> (b n) p d", p=P)
    out_t = out.rearrange("b (n p) d -> (b n) p d", p=P)

    with ExitStack() as ctx:
        def sb(name, cols, dt=F32):
            return ctx.enter_context(nc.sbuf_tensor(name, [P, cols], dt))

        def sem(name):
            return ctx.enter_context(nc.semaphore(name))

        M_hi, M_lo = sb("M_hi", DC * INNER, F32R), sb("M_lo", DC * INNER, F32R)
        N_hi, N_lo = sb("N_hi", PAIRS * D, F32R), sb("N_lo", PAIRS * D, F32R)
        Wq_hi, Wq_lo = sb("Wq_hi", PAIRS * D, F32R), sb("Wq_lo", PAIRS * D, F32R)
        Wo_hi, Wo_lo = sb("Wo_hi", PAIRS * D, F32R), sb("Wo_lo", PAIRS * D, F32R)
        W3_hi, W3_lo = sb("W3_hi", DC * D, F32R), sb("W3_lo", DC * D, F32R)
        bd_hi, bd_lo = sb("bd_hi", PAIRS * P, F32R), sb("bd_lo", PAIRS * P, F32R)
        ku_hi, ku_lo = sb("ku_hi", PAIRS * CTX, F32R), sb("ku_lo", PAIRS * CTX, F32R)
        xT_hi, xT_lo = sb("xT_hi", D, F32R), sb("xT_lo", D, F32R)
        x2T_hi, x2T_lo = sb("x2T_hi", D, F32R), sb("x2T_lo", D, F32R)
        pT_hi, pT_lo = sb("pT_hi", INNER, F32R), sb("pT_lo", INNER, F32R)
        half_ones = [sb(f"half_ones{i}", P, F32R) for i in range(2)]
        ident = sb("ident", P)
        ffn_bias_row = sb("ffn_bias_row", D)
        fs = sb("fs", B * PAIRS)
        F_fac = sb("F_fac", B * PAIRS)
        U_fac = sb("U_fac", B * PAIRS)
        bq = sb("bq", PAIRS)
        minus_half = sb("minus_half", 1)
        zero_col = sb("zero_col", 1)
        bn1, bn2 = sb("bn1", 6), sb("bn2", 6)
        mv1, mv2 = sb("mv1", 2), sb("mv2", 2)
        var1, var2 = sb("var1", 1), sb("var2", 1)
        rs1, rs2 = sb("rs1", 1), sb("rs2", 1)
        row_max = [sb(f"row_max{i}", H) for i in range(2)]
        row_sum = [sb(f"row_sum{i}", H) for i in range(2)]
        row_inv = [sb(f"row_inv{i}", H) for i in range(2)]

        area = sb("area", 15 * D)

        def carve():
            at = [0]

            def take(cols):
                at[0] += cols
                assert at[0] <= 15 * D
                return area[:, at[0] - cols:at[0]]
            return take

        take = carve()
        stage = [take(2 * D) for _ in range(3)]
        ctx_in = [take(D) for _ in range(2)]
        ctx_n = take(D)
        kv_out = [take(D) for _ in range(2)]
        ln1_w_row, ln1_b_row, ln2_w_row, ln2_b_row = (take(D) for _ in range(4))
        take = carve()
        xr = [take(D) for _ in range(RING)]
        S = [take(INNER) for _ in range(2)]
        xn, x2n, hid = take(D), take(D), take(D)
        bias = take(INNER)
        kvf, kus = take(PAIRS * CTX), take(PAIRS * CTX)

        banks = [ctx.enter_context(nc.psum_tensor(f"bank{i}", [P, BANK], F32)) for i in range(8)]
        S_ps, pT_ps = banks[0:2], banks[2:4]
        xT_ps, x2T_ps, O_ps, F_ps = banks[4:8]
        fold_ps = S_ps + pT_ps

        def at_least(eng, s, n):
            if not isinstance(n, int) or n > 0:
                eng.wait_ge(s, n)

        def passes(eng, ps, pairs, wait_lo=None, last=True):
            n = 0
            for sh, _, mh, ml in pairs:
                for mv in (mh, ml):
                    mm = eng.matmul(ps, sh, mv, start=(n == 0), stop=False)
                    n += 1
            if wait_lo:
                wait_lo()
            for k, (_, sl, mh, _) in enumerate(pairs):
                mm = eng.matmul(ps, sl, mh, start=False, stop=(k == len(pairs) - 1))
            return mm

        wk_v = wkv.rearrange("(k p) (s n) -> s k p n", p=P, s=2)
        pairs_of = lambda w: w.rearrange("(g k p) n -> g p k n", p=P, k=2)
        A1, A2, W = pairs_of(aux1T), pairs_of(aux2), pairs_of(ffn_wT)
        WQ, WO = pairs_of(wqT), pairs_of(wout)
        chunks = [(A1[g], M_hi, M_lo, g * 1024, None) for g in range(2)]
        chunks += [(A2[g], Wq_hi, Wq_lo, g * 1024, None) for g in range(2)]
        chunks += [(W[g], M_hi, M_lo, 2048 + g * 1024, None) for g in range(2)]
        chunks += [(wk_v[0, k], Wo_hi, Wo_lo, k * 1024, None) for k in range(4)]
        chunks += [(wk_v[1, k], M_hi, M_lo, k * 1024, "w3") for k in range(4)]
        WQ_FIRST = len(chunks)
        chunks += [(WQ[g], Wq_hi, Wq_lo, g * 1024, "w3") for g in range(4)]
        chunks += [(WO[g], Wo_hi, Wo_lo, g * 1024, "k") for g in range(4)]
        steps = [("split", c) for c in range(4)] + [("ln", 0), ("split", 4), ("split", 5)]
        for m in range(8):
            steps += [("chain", m), ("turn", m)] + [("ln", m + 1)] * (m < 7)
            steps += [("split", 6 + m)] * (m < 4)
        kv_steps = []
        for n in range(32):
            kv_steps += [("kv", n)]
            if n < 8 and n % 2 == 0:
                kv_steps += [("split", 10 + n // 2)]
            if 8 <= n < 16 and n % 2 == 0:
                kv_steps += [("split", 14 + (n - 8) // 2)]
            if 18 <= n < 26 and n % 2 == 0:
                kv_steps += [("split", 18 + (n - 18) // 2)]
        steps += kv_steps
        turn_ps, prod_ps = banks[0:4], banks[4:8]

        s_const = sem("s_const")
        s_rows = sem("s_rows")
        s_stage = [sem(f"s_stage{i}") for i in range(3)]
        s_ctx = [sem(f"s_ctx{i}") for i in range(2)]
        s_fold = sem("s_fold")
        s_shi, s_slo = sem("s_shi"), sem("s_slo")
        s_bn, s_ag, s_cv, s_crs, s_cz0, s_cz = (sem(n) for n in ("s_bn", "s_ag", "s_cv", "s_crs", "s_cz0", "s_cz"))
        s_tp, s_thi, s_tlo = sem("s_tp"), sem("s_thi"), sem("s_tlo")
        s_kv, s_kvo = sem("s_kv"), sem("s_kvo")
        s_kvst = [sem(f"s_kvst{i}") for i in range(2)]
        s_fac = sem("s_fac")
        s_ones = sem("s_ones")

        turn_use = {}
        for st in steps:
            if st[0] in ("chain", "turn"):
                turn_use[st] = len(turn_use)

        with nc.Block() as block:
            @block.sync
            def _(sp):
                for row, dst in ((ln1_w, ln1_w_row), (ln1_b, ln1_b_row), (ln2_w, ln2_w_row),
                                 (ln2_b, ln2_b_row), (ffn_bias, ffn_bias_row[:])):
                    sp.dma_start(dst, row.rearrange("(a n) -> a n", a=1).to_broadcast([P, D])).then_inc(s_rows, 16)
                sp.dma_start(fs[:], fs_cols).then_inc(s_rows, 16)
                sp.dma_start(ident[:], ident_in).then_inc(s_rows, 16)
                for c, (src, *_rest) in enumerate(chunks):
                    at_least(sp, s_slo, c - 2)
                    dst = stage[c % 3]
                    if len(src.shape) == 3:
                        dst = dst.rearrange("p (k n) -> p k n", k=2)
                    sp.dma_start(dst, src).then_inc(s_stage[c % 3], 16)

            @block.gpsimd
            def _(pool):
                pool.memset(minus_half[:], -0.5).then_inc(s_const, 1)
                ctx_t = ctx_rows.rearrange("(n p) d -> n p d", p=P)
                for i in range(2):
                    pool.dma_start(ctx_in[i], ctx_t[i]).then_inc(s_ctx[i], 16)
                pool.wait_ge(s_const, 1)
                for step, i in steps:
                    if step == "ln":
                        pool.wait_ge(s_cv, i + 1)
                        at_least(pool, s_cz, i)
                        pool.tensor_tensor(rs1[:], var1[:], minus_half[:], ALU.pow).then_inc(s_crs, 1)
                        if 1 <= i and i + 1 < 8:
                            pool.wait_ge(s_cz, i)
                            pool.dma_start(ctx_in[(i + 1) % 2], ctx_t[i + 1]).then_inc(s_ctx[(i + 1) % 2], 16)
                    if step == "kv":
                        pool.wait_ge(s_kvo, i + 1)
                        half = i % 2
                        pool.dma_start(kv_scratch[i // 16, (i // 2) % 8, :, half * 8:half * 8 + 8, :],
                                       kv_out[i % 2].rearrange("p (b j) -> p b j", b=8)).then_inc(s_kvst[i % 2], 16)
                for q in s_kvst:
                    pool.wait_ge(q, 16 * 16)

            @block.scalar
            def _(act):
                for step, i in steps:
                    if step == "split":
                        _, hi, _, col, gate = chunks[i]
                        if i >= WQ_FIRST and i < WQ_FIRST + 4:
                            act.wait_ge(s_fold, i - WQ_FIRST + 1)
                        else:
                            act.wait_ge(s_stage[i % 3], 16 * (i // 3 + 1))
                        if gate == "w3":
                            act.wait_ge(s_tp, turn_use[("chain", 7)] + 1)
                        if gate == "k":
                            act.wait_ge(s_kv, 16)
                        act.copy(hi[:, col:col + 1024], stage[i % 3]).then_inc(s_shi, 1)
                    if step in ("chain", "turn"):
                        n = turn_use[(step, i)]
                        act.wait_ge(s_tp, n + 1)
                        if step == "chain":
                            hi = Wq_hi[:, 2048 + i * D:2048 + (i + 1) * D] if i < 4 else W3_hi[:, (i - 4) * D:(i - 3) * D]
                            act.copy(hi, turn_ps[n % 4][:]).then_inc(s_thi, 1)
                        else:
                            hi = N_hi[:, :].rearrange("p (k r) -> p k r", k=DC)[:, :, i * P:(i + 1) * P]
                            act.copy(hi, turn_ps[n % 4][:].rearrange("p (k r) -> p k r", k=DC)).then_inc(s_thi, 1)
                    if step == "kv":
                        act.wait_ge(s_kv, i + 1)
                        at_least(act, s_kvst[i % 2], 16 * (i // 2))
                        act.copy(kv_out[i % 2], prod_ps[i % 4][:]).then_inc(s_kvo, 1)

            @block.vector
            def _(dve):
                dve.memset(zero_col[:], 0.0).then_inc(s_ones, 1)
                for half in range(2):
                    dve.memset(half_ones[half][:].bitcast(F32), 0.0).then_inc(s_ones, 1)
                dve.memset(bd_hi[:].bitcast(F32), 0.0).then_inc(s_ones, 1)
                dve.memset(bd_lo[:].bitcast(F32), 0.0).then_inc(s_ones, 1)
                dve.wait_ge(s_ones, 5)
                for half in range(2):
                    dve.memset(half_ones[half][half * DH:(half + 1) * DH, :].bitcast(F32), 1.0).then_inc(s_ones, 1)
                dve.wait_ge(s_rows, 7 * 16)
                for step, i in steps:
                    if step == "split":
                        _, hi, lo, col, gate = chunks[i]
                        if i >= WQ_FIRST and i < WQ_FIRST + 4:
                            g = i - WQ_FIRST
                            dve.wait_ge(s_stage[i % 3], 16 * (i // 3 + 1))
                            for k in range(2):
                                at_least(dve, s_fac, 2 * g + k)
                                dve.scalar_tensor_tensor(out=ctx_n, in0=stage[i % 3][:, k * D:(k + 1) * D], scalar=1.0,
                                                         in1=ln2_b_row, op0=ALU.mult, op1=ALU.mult,
                                                         accum_out=bq[:, 2 * g + k:2 * g + k + 1]).then_inc(s_fac, 1)
                            dve.wait_ge(s_fac, 2 * g + 2)
                            v = stage[i % 3].rearrange("p (k n) -> p k n", k=2)
                            dve.tensor_tensor(v, v, ln2_w_row.unsqueeze(1).to_broadcast([P, 2, D]),
                                              ALU.mult).then_inc(s_fold, 1)
                        dve.wait_ge(s_shi, i + 1)
                        dve.tensor_tensor(lo[:, col:col + 1024], stage[i % 3], hi[:, col:col + 1024].bitcast(F32),
                                          ALU.subtract).then_inc(s_slo, 1)
                    if step in ("chain", "turn"):
                        n = turn_use[(step, i)]
                        dve.wait_ge(s_thi, n + 1)
                        if step == "chain":
                            a = (Wq_hi, Wq_lo, 2048 + i * D) if i < 4 else (W3_hi, W3_lo, (i - 4) * D)
                            h, l = (y[:, a[2]:a[2] + D] for y in a[:2])
                            ps = turn_ps[n % 4][:]
                        else:
                            h, l = (y[:, :].rearrange("p (k r) -> p k r", k=DC)[:, :, i * P:(i + 1) * P] for y in (N_hi, N_lo))
                            ps = turn_ps[n % 4][:].rearrange("p (k r) -> p k r", k=DC)
                        dve.tensor_tensor(l, ps, h.bitcast(F32), ALU.subtract).then_inc(s_tlo, 1)
                    if step == "ln":
                        dve.wait_ge(s_ctx[i % 2], 16 * (i // 2 + 1))
                        dve.bn_stats(bn1[:], ctx_in[i % 2]).then_inc(s_bn, 1)
                        dve.wait_ge(s_bn, i + 1)
                        dve.bn_aggr(mv1[:], bn1[:]).then_inc(s_ag, 1)
                        dve.wait_ge(s_ag, i + 1)
                        dve.tensor_scalar(var1[:], mv1[:, 1:2], EPS, None, ALU.add).then_inc(s_cv, 1)
                        if i:
                            dve.wait_ge(s_tp, turn_use[("turn", i - 1)] + 1)
                        dve.scalar_tensor_tensor(out=ctx_n, in0=ctx_in[i % 2], scalar=mv1[:, 0:1], in1=ln1_w_row,
                                                 op0=ALU.subtract, op1=ALU.mult).then_inc(s_cz0, 1)
                        dve.wait_ge(s_cz0, i + 1)
                        dve.wait_ge(s_crs, i + 1)
                        dve.scalar_tensor_tensor(out=ctx_n, in0=ctx_n, scalar=rs1[:, 0:1], in1=ln1_b_row,
                                                 op0=ALU.mult, op1=ALU.add).then_inc(s_cz, 1)
                n = [PAIRS]

                def link(ins):
                    n[0] += 1
                    ins.then_inc(s_fac, 1)
                    dve.wait_ge(s_fac, n[0])
                dve.wait_ge(s_fac, PAIRS)
                link(dve.tensor_scalar(F_fac[:], fs[:], SCALE, SCALE, ALU.mult, ALU.add))
                v = lambda a: a[:].rearrange("p (b q) -> p b q", q=PAIRS)
                link(dve.tensor_tensor(v(U_fac), v(F_fac), bq[:].unsqueeze(1).to_broadcast([P, B, PAIRS]), ALU.mult))
                link(dve.scalar_tensor_tensor(out=U_fac[:], in0=fs[:], scalar=SCALE, in1=U_fac[:],
                                              op0=ALU.mult, op1=ALU.add))

            @block.tensor
            def _(pe):
                pe.wait_ge(s_rows, 7 * 16)
                split_of = lambda c: at_least(pe, s_slo, c)
                for step, i in steps:
                    if step == "chain":
                        n = turn_use[(step, i)]
                        at_least(pe, s_tlo, n - 3)
                        if i == 0:
                            split_of(4)
                        if i == 4:
                            split_of(6)
                            pe.wait_ge(s_tlo, turn_use[("chain", 3)] + 1)
                        a, b = (0, 0) if i < 4 else (2048, 2048)
                        m = i % 4
                        st = lambda y, k: y[:, a + k * D + m * P:a + k * D + (m + 1) * P]
                        mo = lambda y, k: y[:, b + k * D:b + (k + 1) * D]
                        passes(pe, turn_ps[n % 4][:], [(st(M_hi, k), st(M_lo, k), mo(Wq_hi, k), mo(Wq_lo, k))
                                                       for k in range(DC)]).then_inc(s_tp, 1)
                    if step == "turn":
                        n = turn_use[(step, i)]
                        at_least(pe, s_tlo, n - 3)
                        pe.wait_ge(s_cz, i + 1)
                        for k in range(DC):
                            tr = pe.transpose(turn_ps[n % 4][:, k * P:(k + 1) * P], ctx_n[:, k * P:(k + 1) * P], ident[:])
                        tr.then_inc(s_tp, 1)
                    if step == "kv":
                        if i == 0:
                            split_of(10)
                            pe.wait_ge(s_tlo, turn_use[("turn", 7)] + 1)
                        if i == 16:
                            split_of(14)
                        at_least(pe, s_kvo, i - 3)
                        w, p, half = (Wo_hi, Wo_lo) if i < 16 else (M_hi, M_lo), (i // 2) % 8, i % 2
                        st = lambda y, k: y[:, k * INNER + p * P:k * INNER + (p + 1) * P]
                        mo = lambda y, k: y[:, k * 1024 + half * BANK:k * 1024 + (half + 1) * BANK]
                        passes(pe, prod_ps[i % 4][:], [(st(w[0], k), st(w[1], k), mo(N_hi, k), mo(N_lo, k))
                                                       for k in range(DC)]).then_inc(s_kv, 1)

        two = lambda name: [sem(f"{name}{i}") for i in range(2)]
        s_xin = [sem(f"s_xin{i}") for i in range(RING)]
        s_xout = [sem(f"s_xout{i}") for i in range(RING)]
        s_kin, s_vin = sem("s_kin"), sem("s_vin")
        s_bn1, s_ag1, s_var1, s_rs1, s_xn = (sem(n) for n in ("s_bn1", "s_ag1", "s_var1", "s_rs1", "s_xn"))
        s_bn2, s_ag2, s_var2, s_rs2, s_x2n = (sem(n) for n in ("s_bn2", "s_ag2", "s_var2", "s_rs2", "s_x2n"))
        s_xT, s_xTh, s_xTl = sem("s_xT"), sem("s_xTh"), sem("s_xTl")
        s_x2T, s_x2Th, s_x2Tl = sem("s_x2T"), sem("s_x2Th"), sem("s_x2Tl")
        s_sc, s_sb, s_mx, s_sub, s_ex = two("s_sc"), two("s_sb"), two("s_mx"), two("s_sub"), two("s_ex")
        s_sum, s_inv, s_p = two("s_sum"), two("s_inv"), two("s_p")
        s_pT, s_pTh, s_pTl = two("s_pT"), two("s_pTh"), two("s_pTl")
        s_o, s_x2, s_f, s_fb, s_th, s_y = (sem(n) for n in ("s_o", "s_x2", "s_f", "s_fb", "s_th", "s_y"))
        s_m, s_mh, s_ml = sem("s_m"), sem("s_mh"), sem("s_ml")
        s_n, s_nh, s_nl = sem("s_n"), sem("s_nh"), sem("s_nl")
        s_bi, s_bs = two("s_bi"), sem("s_bs")
        s_ku, s_ks, s_kuh, s_kh, s_kp = (sem(n) for n in ("s_ku", "s_ks", "s_kuh", "s_kh", "s_kp"))
        s_kul = sem("s_kul")
        s_vh, s_vp = sem("s_vh"), sem("s_vp")

        heads = lambda a: a.rearrange("p (h j) -> p h j", j=CTX)
        half_of = lambda a, q: a[:, q * BANK:(q + 1) * BANK]
        H2 = H // 2

        def diag(y, half):
            return y[half * DH:(half + 1) * DH, :].rearrange("p (q c) -> p q c", c=P)[:, :, half * CTX:(half + 1) * CTX]

        def dense(y, half):
            return y[half * DH:(half + 1) * DH, :].rearrange("p (q j) -> p q j", j=CTX)

        def of_batch(y, b):
            return y[:, bass.ds(b * PAIRS, PAIRS)].unsqueeze(2).to_broadcast([P, PAIRS, CTX])

        def load_x(sp, u, r):
            at_least(sp, s_xout[r], 4 * (u - r) if not isinstance(u, int) else 16 * (u // RING))
            sp.dma_start(xr[r], x_t[bass.ds(u, 1), :, :].rearrange("o p d -> (o p) d")).then_inc(s_xin[r], 16)

        def x_loaded(eng, u, r):
            eng.wait_ge(s_xin[r], 4 * (u - r) + 16)

        def load_kv(sp, which, b, s):
            src = kv_scratch[which].rearrange("q p b j -> b p q j")[bass.ds(b, 1)].rearrange("o p q j -> (o p) q j")
            sp.dma_start(kvf.rearrange("p (q j) -> p q j", j=CTX), src).then_inc(s, 16)

        def load_k(sp, b):
            at_least(sp, s_vp, b)
            load_kv(sp, 0, b, s_kin)

        def load_v(sp, b):
            at_least(sp, s_kp, b + 1)
            load_kv(sp, 1, b, s_vin)

        def k_prepare_pool(pool, b):
            pool.wait_ge(s_kin, 16 * b + 16)
            q = lambda a: a.rearrange("p (q j) -> p q j", j=CTX)
            pool.tensor_tensor(q(kus), q(kvf), of_batch(U_fac, b), ALU.mult).then_inc(s_ku, 1)
            pool.wait_ge(s_ku, b + 1)
            pool.tensor_tensor(q(kvf), q(kvf), of_batch(F_fac, b), ALU.mult).then_inc(s_ks, 1)

        def ku_split_lo(pool, b):
            pool.wait_ge(s_kuh, b + 1)
            pool.tensor_tensor(ku_lo[:], kus, ku_hi[:].bitcast(F32), ALU.subtract).then_inc(s_kul, 1)

        def diag_lo(dve, s_hi, s_done, b):
            dve.wait_ge(s_hi, b + 1)
            for half in range(2):
                last = dve.tensor_tensor(diag(bd_lo, half), dense(kvf, half), diag(bd_hi, half).bitcast(F32), ALU.subtract)
            last.then_inc(s_done, 1)

        def k_prepare_act(act, b):
            at_least(act, s_bi[1], b)
            act.wait_ge(s_ku, b + 1)
            act.copy(ku_hi[:], kus).then_inc(s_kuh, 1)
            at_least(act, s_n, 8 * b)
            act.wait_ge(s_ks, b + 1)
            for half in range(2):
                last = act.copy(diag(bd_hi, half), dense(kvf, half))
            last.then_inc(s_kh, 1)

        def v_prepare_act(act, b):
            act.wait_ge(s_vin, 16 * b + 16)
            act.wait_ge(s_m, 8 * b + 8)
            for half in range(2):
                last = act.copy(diag(bd_hi, half), dense(kvf, half))
            last.then_inc(s_vh, 1)

        def fold_m_pe(pe, b8, free):
            pe.wait_ge(s_kp, b8 // 8 + 1)
            for c in range(8):
                dc, q = c // 2, c % 2
                if c < 4:
                    free(c)
                else:
                    pe.wait_ge(s_ml, b8 + c - 3)
                ps = fold_ps[c % 4]
                for i in range(4):
                    p = 4 * q + i
                    st = lambda y: y[:, p * D + dc * P:p * D + (dc + 1) * P]
                    mo = lambda y: y[:, p * P:(p + 1) * P]
                    mm = passes(pe, ps[:, i * P:(i + 1) * P], [(st(Wq_hi), st(Wq_lo), mo(bd_hi), mo(bd_lo))])
                mm.then_inc(s_m, 1)
            pe.wait_ge(s_kul, b8 // 8 + 1)
            for half in range(2):
                pe.wait_ge(s_ml, b8 + 5 + half)
                pe.matmul(fold_ps[half][:], half_ones[half][:], ku_hi[:], start=True, stop=False)
                pe.matmul(fold_ps[half][:], half_ones[half][:], ku_lo[:], start=False, stop=True).then_inc(s_bi[half], 1)

        def fold_n_pe(pe, b8, free):
            pe.wait_ge(s_vp, b8 // 8 + 1)
            for p in range(PAIRS):
                if p < 4:
                    free(p)
                else:
                    pe.wait_ge(s_nl, b8 + p - 3)
                st = lambda y: y[:, p * P:(p + 1) * P]
                mo = lambda y: y[:, p * D:(p + 1) * D]
                passes(pe, fold_ps[p % 4][:], [(st(bd_hi), st(bd_lo), mo(Wo_hi), mo(Wo_lo))]).then_inc(s_n, 1)

        def m_cols(y, c):
            return y[:, (c // 2) * INNER + (c % 2) * BANK:(c // 2) * INNER + (c % 2 + 1) * BANK]

        def fold_hi(act, b8, produced, done, dst):
            for c in range(8):
                act.wait_ge(produced, b8 + c + 1)
                act.copy(dst(c), fold_ps[c % 4][:]).then_inc(done, 1)

        def fold_lo(dve, b8, produced, done, hi, lo):
            for c in range(8):
                dve.wait_ge(produced, b8 + c + 1)
                dve.tensor_tensor(lo(c), fold_ps[c % 4][:], hi(c).bitcast(F32), ALU.subtract).then_inc(done, 1)

        def bias_copy(dve, b8):
            for half in range(2):
                dve.wait_ge(s_bi[half], b8 // 8 + 1)
                last = dve.tensor_copy(bias.rearrange("p (q s j) -> p q s j", s=2, j=CTX)[:, :, half, :],
                                       fold_ps[half][:].rearrange("p (q j) -> p q j", j=CTX))
            last.then_inc(s_bs, 1)

        n_cols = lambda y, c: y[:, c * D:(c + 1) * D]
        M_fold = (s_mh, s_ml, lambda c: m_cols(M_hi, c), lambda c: m_cols(M_lo, c))
        N_fold = (s_nh, s_nl, lambda c: n_cols(N_hi, c), lambda c: n_cols(N_lo, c))

        def layernorm_stats(dve, src, bn, mv, var, s_bn_, s_ag_, s_var_, u, mul, add, between=None):
            dve.bn_stats(bn[:], src).then_inc(s_bn_, 1)
            dve.wait_ge(s_bn_, u + 1)
            if between:
                between()
            dve.bn_aggr(mv[:], bn[:]).then_inc(s_ag_, 1)
            dve.wait_ge(s_ag_, u + 1)
            dve.tensor_scalar(var[:], mv[:, 1:2], mul, add, ALU.mult, ALU.add).then_inc(s_var_, 1)

        def turn(pe, ps, src, s):
            for k in range(4):
                tr = pe.transpose(ps[:, k * P:(k + 1) * P], src[:, k * P:(k + 1) * P], ident[:])
            tr.then_inc(s, 1)

        def ln1_stats(dve, u, r, between=None):
            x_loaded(dve, u, r)
            layernorm_stats(dve, xr[r], bn1, mv1, var1, s_bn1, s_ag1, s_var1, u, 1.0 + EPS,
                            EPS * EPS, between)

        def ln1_apply(dve, u, r):
            dve.wait_ge(s_rs1, u + 1)
            at_least(dve, s_xT, u)
            dve.tensor_scalar(xn, xr[r], mv1[:, 0:1], rs1[:, 0:1], ALU.subtract, ALU.mult).then_inc(s_xn, 1)

        def pow1(pool, u):
            pool.wait_ge(s_var1, u + 1)
            at_least(pool, s_xn, u)
            pool.tensor_tensor(rs1[:], var1[:], minus_half[:], ALU.pow).then_inc(s_rs1, 1)

        def turn_xn(pe, u):
            pe.wait_ge(s_xn, u + 1)
            turn(pe, xT_ps, xn, s_xT)

        def xT_split_hi(act, u):
            act.wait_ge(s_xT, u + 1)
            at_least(act, s_sc[1], u)
            act.copy(xT_hi[:], xT_ps[:]).then_inc(s_xTh, 1)

        def xT_split_lo(dve, u):
            dve.wait_ge(s_xTh, u + 1)
            at_least(dve, s_sc[1], u)
            dve.tensor_tensor(xT_lo[:], xT_ps[:], xT_hi[:].bitcast(F32), ALU.subtract).then_inc(s_xTl, 1)

        def parts(t, m, first):
            known = isinstance(t, int)
            return dict(scores=not known or t < T, following=not known or t + 1 < T,
                        attn=not known or 1 <= t <= T, chain=not known or t >= 2,
                        fold_m=m == 7 and (not known or t + 1 < T), fold_n=m == 0 and (not known or 0 < t < T),
                        more=not known or t + TPB < T)

        def slot_sp(sp, t, m):
            has = parts(t, m, False)
            if has["more"] and m == 2:
                load_k(sp, (t + 6) // 8)
            if has["more"] and m == 5:
                load_v(sp, (t + 3) // 8)
            if has["chain"]:
                sp.wait_ge(s_y, t - 1)
                r = (m - 2) % RING
                sp.dma_start(out_t[bass.ds(t - 2, 1), :, :].rearrange("o p d -> (o p) d"), xr[r]).then_inc(s_xout[r], 16)
            if not isinstance(t, int) or t + 2 < T:
                load_x(sp, t + 2, (m + 2) % RING)

        def slot_pe(pe, t, m):
            has = parts(t, m, False)
            if has["scores"]:
                pe.wait_ge(s_xTh, t + 1)
                if m == 0:
                    pe.wait_ge(s_ml, t + 8)
                    pe.wait_ge(s_bs, t // 8 + 1)
                if m == 1:
                    pe.wait_ge(s_nl, t + 7)
                for q in range(2):
                    at_least(pe, s_sb[q], t)
                    mo = lambda y, k: y[:, k * INNER + q * BANK:k * INNER + (q + 1) * BANK]
                    st = lambda y, k: y[:, k * P:(k + 1) * P]
                    passes(pe, S_ps[q][:], [(st(xT_hi, k), st(xT_lo, k), mo(M_hi, k), mo(M_lo, k)) for k in range(DC)],
                           (lambda: pe.wait_ge(s_xTl, t + 1)) if q == 0 else None).then_inc(s_sc[q], 1)
            if has["chain"]:
                pe.wait_ge(s_x2n, t - 1)
                at_least(pe, s_x2Tl, t - 2)
                turn(pe, x2T_ps, x2n, s_x2T)
            if has["attn"]:
                for q in range(2):
                    pe.wait_ge(s_p[q], t)
                    at_least(pe, s_pTl[q], t - 1)
                    turn(pe, pT_ps[q], half_of(S[(m - 1) % 2], q), s_pT[q])
            if has["chain"]:
                pe.wait_ge(s_x2Th, t - 1)
                at_least(pe, s_fb, t - 2)
                st = lambda y, k: y[:, k * P:(k + 1) * P]
                mo = lambda y, k: y[:, k * D:(k + 1) * D]
                passes(pe, F_ps[:], [(st(x2T_hi, k), st(x2T_lo, k), mo(W3_hi, k), mo(W3_lo, k)) for k in range(DC)],
                       lambda: pe.wait_ge(s_x2Tl, t - 1)).then_inc(s_f, 1)
            if has["fold_m"]:
                fold_m_pe(pe, t + 1, lambda c: pe.wait_ge(s_sb[c], t + 1) if c < 2 else pe.wait_ge(s_pTl[c - 2], t))
            if has["attn"]:
                at_least(pe, s_x2, t - 1)
                for q in range(2):
                    pe.wait_ge(s_pTh[q], t)
                    ks = range(4 * q, 4 * q + 4)
                    for k in ks:
                        for mv in (N_hi, N_lo):
                            pe.matmul(O_ps[:], pT_hi[:, k * P:(k + 1) * P], n_cols(mv, k),
                                      start=(k == 0 and mv is N_hi), stop=False)
                    pe.wait_ge(s_pTl[q], t)
                    for k in ks:
                        mm = pe.matmul(O_ps[:], pT_lo[:, k * P:(k + 1) * P], n_cols(N_hi, k), start=False, stop=(k == 7))
                    if q == 0 and has["following"]:
                        turn_xn(pe, t + 1)
                mm.then_inc(s_o, 1)
            elif has["following"]:
                turn_xn(pe, t + 1)
            if has["fold_n"]:
                fold_n_pe(pe, t, lambda c: pe.wait_ge(s_sb[c], t + 1) if c < 2 else None)

        def slot_act(act, t, m):
            has = parts(t, m, False)

            def exp(q):
                act.wait_ge(s_sub[q], t + 1)
                s = half_of(S[m % 2], q)
                act.activation(s, s, ACT.Exp).then_inc(s_ex[q], 1)

            if has["scores"]:
                exp(0)
            if has["chain"]:
                act.wait_ge(s_x2T, t - 1)
                at_least(act, s_f, t - 2)
                act.copy(x2T_hi[:], x2T_ps[:]).then_inc(s_x2Th, 1)
            if has["attn"]:
                at_least(act, s_o, t - 1)
                for q in range(2):
                    act.wait_ge(s_pT[q], t)
                    act.copy(half_of(pT_hi, q), pT_ps[q][:]).then_inc(s_pTh[q], 1)
            if has["scores"]:
                exp(1)
            if has["fold_n"]:
                v_prepare_act(act, t // 8)
            if has["more"] and m == 4:
                k_prepare_act(act, (t + 4) // 8)
            if has["chain"]:
                act.wait_ge(s_fb, t - 1)
                act.activation(hid, hid, ACT.Tanh).then_inc(s_th, 1)
            if has["fold_m"]:
                fold_hi(act, t + 1, s_m, s_mh, M_fold[2])
            if has["following"]:
                xT_split_hi(act, t + 1)
            if has["fold_n"]:
                fold_hi(act, t, s_n, s_nh, N_fold[2])

        def slot_dve(dve, t, m):
            has = parts(t, m, False)
            r2 = (m - 2) % RING

            def read_scores(q):
                dve.wait_ge(s_sc[q], t + 1)
                at_least(dve, s_pT[q], t - 1)
                if m == 0 and q == 0:
                    dve.wait_ge(s_bs, t // 8 + 1)
                dve.tensor_tensor(half_of(S[m % 2], q), S_ps[q][:], half_of(bias, q), ALU.add).then_inc(s_sb[q], 1)

            def maximum(q):
                dve.wait_ge(s_sb[q], t + 1)
                dve.tensor_reduce(row_max[m % 2][:, q * H2:(q + 1) * H2], heads(half_of(S[m % 2], q)), AX_X,
                                  ALU.max).then_inc(s_mx[q], 1)

            if has["chain"]:
                dve.wait_ge(s_o, t - 1)
                dve.tensor_tensor(xr[r2], O_ps[:], xr[r2], ALU.add).then_inc(s_x2, 1)
                dve.wait_ge(s_x2, t - 1)
                layernorm_stats(dve, xr[r2], bn2, mv2, var2, s_bn2, s_ag2, s_var2, t - 2, 1.0, EPS,
                                (lambda: read_scores(0)) if has["scores"] else None)
            elif has["scores"]:
                read_scores(0)
            if has["chain"]:
                dve.wait_ge(s_rs2, t - 1)
                at_least(dve, s_x2T, t - 2)
                dve.tensor_scalar(x2n, xr[r2], mv2[:, 0:1], rs2[:, 0:1], ALU.subtract, ALU.mult).then_inc(s_x2n, 1)
            if has["scores"]:
                maximum(0)
            if has["following"]:
                ln1_stats(dve, t + 1, (m + 1) % RING, lambda: read_scores(1))
            elif has["scores"]:
                read_scores(1)
            if has["scores"]:
                maximum(1)
            if has["following"]:
                ln1_apply(dve, t + 1, (m + 1) % RING)
            if has["chain"]:
                dve.wait_ge(s_x2Th, t - 1)
                at_least(dve, s_f, t - 2)
                dve.tensor_tensor(x2T_lo[:], x2T_ps[:], x2T_hi[:].bitcast(F32), ALU.subtract).then_inc(s_x2Tl, 1)
            if has["attn"]:
                at_least(dve, s_o, t - 1)
                for q in range(2):
                    dve.wait_ge(s_pTh[q], t)
                    dve.tensor_tensor(half_of(pT_lo, q), pT_ps[q][:], half_of(pT_hi, q).bitcast(F32),
                                      ALU.subtract).then_inc(s_pTl[q], 1)
            if has["fold_n"]:
                diag_lo(dve, s_vh, s_vp, t // 8)
            if has["scores"]:
                for q in range(2):
                    hs = slice(q * H2, (q + 1) * H2)
                    dve.wait_ge(s_ex[q], t + 1)
                    dve.tensor_reduce(row_sum[m % 2][:, hs], heads(half_of(S[m % 2], q)), AX_X, ALU.add).then_inc(s_sum[q], 1)
                    dve.wait_ge(s_sum[q], t + 1)
                    dve.reciprocal(row_inv[m % 2][:, hs], row_sum[m % 2][:, hs]).then_inc(s_inv[q], 1)
            if has["chain"]:
                dve.wait_ge(s_f, t - 1)
                at_least(dve, s_y, t - 2)
                dve.tensor_tensor(hid, F_ps[:], ffn_bias_row[:], ALU.add).then_inc(s_fb, 1)
            if has["more"] and m == 4:
                diag_lo(dve, s_kh, s_kp, (t + 4) // 8)
            if has["fold_m"]:
                fold_lo(dve, t + 1, *M_fold)
                bias_copy(dve, t + 1)
            if has["following"]:
                xT_split_lo(dve, t + 1)
            if has["fold_n"]:
                fold_lo(dve, t, *N_fold)

        def slot_pool(pool, t, m):
            has = parts(t, m, False)

            def by_head(q, row, op, s_wait, s_done):
                s = heads(half_of(S[m % 2], q))
                pool.wait_ge(s_wait[q], t + 1)
                pool.tensor_tensor(s, s, row[m % 2][:, q * H2:(q + 1) * H2].unsqueeze(2).to_broadcast([P, H2, CTX]),
                                   op).then_inc(s_done[q], 1)

            if has["chain"]:
                pool.wait_ge(s_var2, t - 1)
                at_least(pool, s_x2n, t - 2)
                pool.tensor_tensor(rs2[:], var2[:], minus_half[:], ALU.pow).then_inc(s_rs2, 1)
            if has["scores"]:
                by_head(0, row_max, ALU.subtract, s_mx, s_sub)
            if has["following"]:
                pow1(pool, t + 1)
            if has["scores"]:
                by_head(1, row_max, ALU.subtract, s_mx, s_sub)
            if has["scores"]:
                by_head(0, row_inv, ALU.mult, s_inv, s_p)
                by_head(1, row_inv, ALU.mult, s_inv, s_p)
            if has["chain"]:
                r2 = (m - 2) % RING
                pool.wait_ge(s_th, t - 1)
                pool.tensor_tensor(xr[r2], xr[r2], hid, ALU.add).then_inc(s_y, 1)
            if has["more"] and m == 3:
                k_prepare_pool(pool, (t + 5) // 8)
            if has["more"] and m == 4:
                ku_split_lo(pool, (t + 4) // 8)

        def run(eng, slot):
            for t in range(2):
                slot(eng, t, t)
            with eng.Fori(0, B - 1) as b:
                for j in range(2, TPB + 2):
                    slot(eng, b * TPB + j, j % TPB)
            for t in range(T - 6, T + 2):
                slot(eng, t, t % TPB)

        with nc.Block() as block:
            @block.sync
            def _(sp):
                load_x(sp, 0, 0)
                load_k(sp, 0)
                load_x(sp, 1, 1)
                load_v(sp, 0)
                run(sp, slot_sp)
                for r in range(RING):
                    sp.wait_ge(s_xout[r], 16 * (T // RING))

            @block.tensor
            def _(pe):
                turn_xn(pe, 0)
                fold_m_pe(pe, 0, lambda c: None)
                fold_n_pe(pe, 0, lambda c: pe.wait_ge(s_bs, 1) if c == 0 else pe.wait_ge(s_ml, 8))
                pe.wait_ge(s_nl, 8)
                run(pe, slot_pe)

            @block.scalar
            def _(act):
                k_prepare_act(act, 0)
                xT_split_hi(act, 0)
                fold_hi(act, 0, s_m, s_mh, M_fold[2])
                v_prepare_act(act, 0)
                fold_hi(act, 0, s_n, s_nh, N_fold[2])
                run(act, slot_act)

            @block.vector
            def _(dve):
                ln1_stats(dve, 0, 0)
                ln1_apply(dve, 0, 0)
                diag_lo(dve, s_kh, s_kp, 0)
                xT_split_lo(dve, 0)
                fold_lo(dve, 0, *M_fold)
                bias_copy(dve, 0)
                diag_lo(dve, s_vh, s_vp, 0)
                fold_lo(dve, 0, *N_fold)
                run(dve, slot_dve)

            @block.gpsimd
            def _(pool):
                pow1(pool, 0)
                k_prepare_pool(pool, 0)
                ku_split_lo(pool, 0)
                run(pool, slot_pool)


def kernel(x, ctx_1024, fside_Bx16_0, L0_xattn_ln1_w, L0_xattn_ln1_b, L0_xattn_ln2_w, L0_xattn_ln2_b,
           L0_xattn_Wq, L0_xattn_Wkv, L0_xattn_Wout, L0_ffn_weight, L0_ffn_aux_weight1, L0_ffn_aux_weight2,
           L0_ffn_bias):
    import concourse.bacc as bacc
    from concourse.bass_utils import run_bass_kernel_spmd

    fs_cols = np.ascontiguousarray(
        np.repeat(np.asarray(fside_Bx16_0).reshape(B, PAIRS, 2).transpose(2, 0, 1).reshape(2, 1, B * PAIRS), P // 2, axis=1)
        .reshape(P, B * PAIRS))
    arrays = {
        "x": np.ascontiguousarray(x),
        "ctx_rows": np.ascontiguousarray(np.asarray(ctx_1024).reshape(B * CTX, D)),
        "fs_cols": fs_cols,
        "ln1_w": np.ascontiguousarray(L0_xattn_ln1_w), "ln1_b": np.ascontiguousarray(L0_xattn_ln1_b),
        "ln2_w": np.ascontiguousarray(L0_xattn_ln2_w), "ln2_b": np.ascontiguousarray(L0_xattn_ln2_b),
        "wqT": np.ascontiguousarray(np.asarray(L0_xattn_Wq).T),
        "wkv": np.ascontiguousarray(L0_xattn_Wkv), "wout": np.ascontiguousarray(L0_xattn_Wout),
        "ffn_wT": np.ascontiguousarray(np.asarray(L0_ffn_weight).T),
        "aux1T": np.ascontiguousarray(np.asarray(L0_ffn_aux_weight1).T),
        "aux2": np.ascontiguousarray(L0_ffn_aux_weight2),
        "ffn_bias": np.ascontiguousarray(L0_ffn_bias),
        "ident_in": np.eye(P, dtype=np.float32),
    }
    nc = bacc.Bacc("TRN2", target_bir_lowering=False, num_devices=1)
    args = [nc.dram_tensor(f"{name}_dram", a.shape, mybir.dt.from_np(a.dtype), kind="ExternalInput").ap()
            for name, a in arrays.items()]
    out = nc.dram_tensor("y_dram", (B, ROWS, D), F32, kind="ExternalOutput").ap()
    build(nc, *args, out)
    r = run_bass_kernel_spmd(nc, [{f"{name}_dram": a for name, a in arrays.items()}], core_ids=[0])
    return r.results[0]["y_dram"]
```

```python
from contextlib import ExitStack

import numpy as np

import concourse.bass as bass
from concourse import mybir

F32 = mybir.dt.float32
F32R = mybir.dt.float32r
ALU = mybir.AluOpType
ACT = mybir.ActivationFunctionType
AX_X = mybir.AxisListType.X

P = 128
BANK = 512
EPS = 1e-5
B, ROWS, D = 16, 1024, 512
CTX, H, DH = 64, 16, 64
INNER = H * DH
PAIRS = H // 2
DC = D // P
TPB = ROWS // P
T = B * TPB
RING = 4
SCALE = DH ** -0.5
assert DH == CTX == P // 2 and D == BANK and INNER == 2 * BANK and TPB == 8 and TPB % RING == 0


def build(nc, x, ctx_rows, fs_cols, ln1_w, ln1_b, ln2_w, ln2_b, wqT, wkv, wout, ffn_wT, aux1T, aux2,
          ffn_bias, ident_in, out):
    kv_scratch = nc.dram_tensor("kv_scratch", (2, PAIRS, P, B, CTX), F32, kind="Internal").ap()
    x_t = x.rearrange("b (n p) d -> (b n) p d", p=P)
    out_t = out.rearrange("b (n p) d -> (b n) p d", p=P)

    with ExitStack() as ctx:
        def sb(name, cols, dt=F32):
            return ctx.enter_context(nc.sbuf_tensor(name, [P, cols], dt))

        def sem(name):
            return ctx.enter_context(nc.semaphore(name))

        M_hi, M_lo = sb("M_hi", DC * INNER, F32R), sb("M_lo", DC * INNER, F32R)
        N_hi, N_lo = sb("N_hi", PAIRS * D, F32R), sb("N_lo", PAIRS * D, F32R)
        Wq_hi, Wq_lo = sb("Wq_hi", PAIRS * D, F32R), sb("Wq_lo", PAIRS * D, F32R)
        Wo_hi, Wo_lo = sb("Wo_hi", PAIRS * D, F32R), sb("Wo_lo", PAIRS * D, F32R)
        W3_hi, W3_lo = sb("W3_hi", DC * D, F32R), sb("W3_lo", DC * D, F32R)
        bd = sb("bd", PAIRS * 2 * P, F32R)
        ku_hi, ku_lo = sb("ku_hi", PAIRS * CTX, F32R), sb("ku_lo", PAIRS * CTX, F32R)
        xT_hi, xT_lo = sb("xT_hi", D, F32R), sb("xT_lo", D, F32R)
        x2T_hi, x2T_lo = sb("x2T_hi", D, F32R), sb("x2T_lo", D, F32R)
        pT_hi, pT_lo = sb("pT_hi", INNER, F32R), sb("pT_lo", INNER, F32R)
        half_ones = [sb(f"half_ones{i}", P, F32R) for i in range(2)]
        ident = sb("ident", P)
        ffn_bias_row = sb("ffn_bias_row", D)
        fs = sb("fs", B * PAIRS)
        F_fac = sb("F_fac", B * PAIRS)
        U_fac = sb("U_fac", B * PAIRS)
        bq = sb("bq", PAIRS)
        minus_half = sb("minus_half", 1)
        zero_col = sb("zero_col", 1)
        bn1, bn2 = sb("bn1", 6), sb("bn2", 6)
        mv1, mv2 = sb("mv1", 2), sb("mv2", 2)
        var1, var2 = sb("var1", 1), sb("var2", 1)
        rs1, rs2 = sb("rs1", 1), sb("rs2", 1)
        row_max = [sb(f"row_max{i}", H) for i in range(2)]
        row_sum = [sb(f"row_sum{i}", H) for i in range(2)]
        row_inv = [sb(f"row_inv{i}", H) for i in range(2)]

        area = sb("area", 15 * D)

        def carve():
            at = [0]

            def take(cols):
                at[0] += cols
                assert at[0] <= 15 * D
                return area[:, at[0] - cols:at[0]]
            return take

        take = carve()
        stage = [take(2 * D) for _ in range(3)]
        ctx_in = [take(D) for _ in range(2)]
        ctx_n = take(D)
        kv_out = [take(D) for _ in range(2)]
        ln1_w_row, ln1_b_row, ln2_w_row, ln2_b_row = (take(D) for _ in range(4))
        take = carve()
        xr = [take(D) for _ in range(RING)]
        S = [take(INNER) for _ in range(2)]
        xn, x2n, hid = take(D), take(D), take(D)
        bias = take(INNER)
        kvf, kus = take(PAIRS * CTX), take(PAIRS * CTX)
        m_rest_v, m_cross, m_rest_g = ([y[:, i * 2 * P:(i + 1) * 2 * P] for i in range(2)]
                                       for y in (kus, S[0][:, 0:BANK], S[0][:, BANK:INNER]))

        banks = [ctx.enter_context(nc.psum_tensor(f"bank{i}", [P, BANK], F32)) for i in range(8)]
        S_ps, pT_ps = banks[0:2], banks[2:4]
        xT_ps, x2T_ps, O_ps, F_ps = banks[4:8]
        fold_ps = S_ps + pT_ps
        bias_ps = (O_ps, xT_ps)

        def at_least(eng, s, n):
            if not isinstance(n, int) or n > 0:
                eng.wait_ge(s, n)

        def passes(eng, ps, pairs, wait_lo=None, last=True):
            n = 0
            for sh, _, mh, ml in pairs:
                for mv in (mh, ml):
                    mm = eng.matmul(ps, sh, mv, start=(n == 0), stop=False)
                    n += 1
            if wait_lo:
                wait_lo()
            for k, (_, sl, mh, _) in enumerate(pairs):
                mm = eng.matmul(ps, sl, mh, start=False, stop=(k == len(pairs) - 1))
            return mm

        wk_v = wkv.rearrange("(k p) (s n) -> s k p n", p=P, s=2)
        pairs_of = lambda w: w.rearrange("(g k p) n -> g p k n", p=P, k=2)
        A1, A2, W = pairs_of(aux1T), pairs_of(aux2), pairs_of(ffn_wT)
        WQ, WO = pairs_of(wqT), pairs_of(wout)
        chunks = [(A1[g], M_hi, M_lo, g * 1024, None) for g in range(2)]
        chunks += [(A2[g], Wq_hi, Wq_lo, g * 1024, None) for g in range(2)]
        chunks += [(W[g], M_hi, M_lo, 2048 + g * 1024, None) for g in range(2)]
        chunks += [(wk_v[0, k], Wo_hi, Wo_lo, k * 1024, None) for k in range(4)]
        chunks += [(wk_v[1, k], M_hi, M_lo, k * 1024, "w3") for k in range(4)]
        WQ_FIRST = len(chunks)
        chunks += [(WQ[g], Wq_hi, Wq_lo, g * 1024, "w3") for g in range(4)]
        chunks += [(WO[g], Wo_hi, Wo_lo, g * 1024, "k") for g in range(4)]
        steps = [("split", c) for c in range(4)] + [("ln", 0), ("split", 4), ("split", 5)]
        for m in range(8):
            steps += [("chain", m), ("turn", m)] + [("ln", m + 1)] * (m < 7)
            steps += [("split", 6 + m)] * (m < 4)
        kv_steps = []
        for n in range(32):
            kv_steps += [("kv", n)]
            if n < 8 and n % 2 == 0:
                kv_steps += [("split", 10 + n // 2)]
            if 8 <= n < 16 and n % 2 == 0:
                kv_steps += [("split", 14 + (n - 8) // 2)]
            if 18 <= n < 26 and n % 2 == 0:
                kv_steps += [("split", 18 + (n - 18) // 2)]
        steps += kv_steps
        turn_ps, prod_ps = banks[0:4], banks[4:8]

        s_const = sem("s_const")
        s_rows = sem("s_rows")
        s_stage = [sem(f"s_stage{i}") for i in range(3)]
        s_ctx = [sem(f"s_ctx{i}") for i in range(2)]
        s_fold = sem("s_fold")
        s_shi, s_slo = sem("s_shi"), sem("s_slo")
        s_bn, s_ag, s_cv, s_crs, s_cz0, s_cz = (sem(n) for n in ("s_bn", "s_ag", "s_cv", "s_crs", "s_cz0", "s_cz"))
        s_tp, s_thi, s_tlo = sem("s_tp"), sem("s_thi"), sem("s_tlo")
        s_kv, s_kvo = sem("s_kv"), sem("s_kvo")
        s_kvst = [sem(f"s_kvst{i}") for i in range(2)]
        s_fac = sem("s_fac")
        s_ones = sem("s_ones")

        turn_use = {}
        for st in steps:
            if st[0] in ("chain", "turn"):
                turn_use[st] = len(turn_use)

        with nc.Block() as block:
            @block.sync
            def _(sp):
                for row, dst in ((ln1_w, ln1_w_row), (ln1_b, ln1_b_row), (ln2_w, ln2_w_row),
                                 (ln2_b, ln2_b_row), (ffn_bias, ffn_bias_row[:])):
                    sp.dma_start(dst, row.rearrange("(a n) -> a n", a=1).to_broadcast([P, D])).then_inc(s_rows, 16)
                sp.dma_start(fs[:], fs_cols).then_inc(s_rows, 16)
                sp.dma_start(ident[:], ident_in).then_inc(s_rows, 16)
                for c, (src, *_rest) in enumerate(chunks):
                    at_least(sp, s_slo, c - 2)
                    dst = stage[c % 3]
                    if len(src.shape) == 3:
                        dst = dst.rearrange("p (k n) -> p k n", k=2)
                    sp.dma_start(dst, src).then_inc(s_stage[c % 3], 16)

            @block.gpsimd
            def _(pool):
                pool.memset(minus_half[:], -0.5).then_inc(s_const, 1)
                ctx_t = ctx_rows.rearrange("(n p) d -> n p d", p=P)
                for i in range(2):
                    pool.dma_start(ctx_in[i], ctx_t[i]).then_inc(s_ctx[i], 16)
                pool.wait_ge(s_const, 1)
                for step, i in steps:
                    if step == "ln":
                        pool.wait_ge(s_cv, i + 1)
                        at_least(pool, s_cz, i)
                        pool.tensor_tensor(rs1[:], var1[:], minus_half[:], ALU.pow).then_inc(s_crs, 1)
                        if 1 <= i and i + 1 < 8:
                            pool.wait_ge(s_cz, i)
                            pool.dma_start(ctx_in[(i + 1) % 2], ctx_t[i + 1]).then_inc(s_ctx[(i + 1) % 2], 16)
                    if step == "kv":
                        pool.wait_ge(s_kvo, i + 1)
                        half = i % 2
                        pool.dma_start(kv_scratch[i // 16, (i // 2) % 8, :, half * 8:half * 8 + 8, :],
                                       kv_out[i % 2].rearrange("p (b j) -> p b j", b=8)).then_inc(s_kvst[i % 2], 16)
                for q in s_kvst:
                    pool.wait_ge(q, 16 * 16)

            @block.scalar
            def _(act):
                for step, i in steps:
                    if step == "split":
                        _, hi, _, col, gate = chunks[i]
                        if i >= WQ_FIRST and i < WQ_FIRST + 4:
                            act.wait_ge(s_fold, i - WQ_FIRST + 1)
                        else:
                            act.wait_ge(s_stage[i % 3], 16 * (i // 3 + 1))
                        if gate == "w3":
                            act.wait_ge(s_tp, turn_use[("chain", 7)] + 1)
                        if gate == "k":
                            act.wait_ge(s_kv, 16)
                        act.copy(hi[:, col:col + 1024], stage[i % 3]).then_inc(s_shi, 1)
                    if step in ("chain", "turn"):
                        n = turn_use[(step, i)]
                        act.wait_ge(s_tp, n + 1)
                        if step == "chain":
                            hi = Wq_hi[:, 2048 + i * D:2048 + (i + 1) * D] if i < 4 else W3_hi[:, (i - 4) * D:(i - 3) * D]
                            act.copy(hi, turn_ps[n % 4][:]).then_inc(s_thi, 1)
                        else:
                            hi = N_hi[:, :].rearrange("p (k r) -> p k r", k=DC)[:, :, i * P:(i + 1) * P]
                            act.copy(hi, turn_ps[n % 4][:].rearrange("p (k r) -> p k r", k=DC)).then_inc(s_thi, 1)
                    if step == "kv":
                        act.wait_ge(s_kv, i + 1)
                        at_least(act, s_kvst[i % 2], 16 * (i // 2))
                        act.copy(kv_out[i % 2], prod_ps[i % 4][:]).then_inc(s_kvo, 1)

            @block.vector
            def _(dve):
                dve.memset(zero_col[:], 0.0).then_inc(s_ones, 1)
                for half in range(2):
                    dve.memset(half_ones[half][:].bitcast(F32), 0.0).then_inc(s_ones, 1)
                dve.memset(bd[:].bitcast(F32), 0.0).then_inc(s_ones, 1)
                dve.wait_ge(s_ones, 4)
                for half in range(2):
                    dve.memset(half_ones[half][half * DH:(half + 1) * DH, :].bitcast(F32), 1.0).then_inc(s_ones, 1)
                dve.wait_ge(s_rows, 7 * 16)
                for step, i in steps:
                    if step == "split":
                        _, hi, lo, col, gate = chunks[i]
                        if i >= WQ_FIRST and i < WQ_FIRST + 4:
                            g = i - WQ_FIRST
                            dve.wait_ge(s_stage[i % 3], 16 * (i // 3 + 1))
                            for k in range(2):
                                at_least(dve, s_fac, 2 * g + k)
                                dve.scalar_tensor_tensor(out=ctx_n, in0=stage[i % 3][:, k * D:(k + 1) * D], scalar=1.0,
                                                         in1=ln2_b_row, op0=ALU.mult, op1=ALU.mult,
                                                         accum_out=bq[:, 2 * g + k:2 * g + k + 1]).then_inc(s_fac, 1)
                            dve.wait_ge(s_fac, 2 * g + 2)
                            v = stage[i % 3].rearrange("p (k n) -> p k n", k=2)
                            dve.tensor_tensor(v, v, ln2_w_row.unsqueeze(1).to_broadcast([P, 2, D]),
                                              ALU.mult).then_inc(s_fold, 1)
                        dve.wait_ge(s_shi, i + 1)
                        dve.tensor_tensor(lo[:, col:col + 1024], stage[i % 3], hi[:, col:col + 1024].bitcast(F32),
                                          ALU.subtract).then_inc(s_slo, 1)
                    if step in ("chain", "turn"):
                        n = turn_use[(step, i)]
                        dve.wait_ge(s_thi, n + 1)
                        if step == "chain":
                            a = (Wq_hi, Wq_lo, 2048 + i * D) if i < 4 else (W3_hi, W3_lo, (i - 4) * D)
                            h, l = (y[:, a[2]:a[2] + D] for y in a[:2])
                            ps = turn_ps[n % 4][:]
                        else:
                            h, l = (y[:, :].rearrange("p (k r) -> p k r", k=DC)[:, :, i * P:(i + 1) * P] for y in (N_hi, N_lo))
                            ps = turn_ps[n % 4][:].rearrange("p (k r) -> p k r", k=DC)
                        dve.tensor_tensor(l, ps, h.bitcast(F32), ALU.subtract).then_inc(s_tlo, 1)
                    if step == "ln":
                        dve.wait_ge(s_ctx[i % 2], 16 * (i // 2 + 1))
                        dve.bn_stats(bn1[:], ctx_in[i % 2]).then_inc(s_bn, 1)
                        dve.wait_ge(s_bn, i + 1)
                        dve.bn_aggr(mv1[:], bn1[:]).then_inc(s_ag, 1)
                        dve.wait_ge(s_ag, i + 1)
                        dve.tensor_scalar(var1[:], mv1[:, 1:2], EPS, None, ALU.add).then_inc(s_cv, 1)
                        if i:
                            dve.wait_ge(s_tp, turn_use[("turn", i - 1)] + 1)
                        dve.scalar_tensor_tensor(out=ctx_n, in0=ctx_in[i % 2], scalar=mv1[:, 0:1], in1=ln1_w_row,
                                                 op0=ALU.subtract, op1=ALU.mult).then_inc(s_cz0, 1)
                        dve.wait_ge(s_cz0, i + 1)
                        dve.wait_ge(s_crs, i + 1)
                        dve.scalar_tensor_tensor(out=ctx_n, in0=ctx_n, scalar=rs1[:, 0:1], in1=ln1_b_row,
                                                 op0=ALU.mult, op1=ALU.add).then_inc(s_cz, 1)
                n = [PAIRS]

                def link(ins):
                    n[0] += 1
                    ins.then_inc(s_fac, 1)
                    dve.wait_ge(s_fac, n[0])
                dve.wait_ge(s_fac, PAIRS)
                link(dve.tensor_scalar(F_fac[:], fs[:], SCALE, SCALE, ALU.mult, ALU.add))
                v = lambda a: a[:].rearrange("p (b q) -> p b q", q=PAIRS)
                link(dve.tensor_tensor(v(U_fac), v(F_fac), bq[:].unsqueeze(1).to_broadcast([P, B, PAIRS]), ALU.mult))
                link(dve.scalar_tensor_tensor(out=U_fac[:], in0=fs[:], scalar=SCALE, in1=U_fac[:],
                                              op0=ALU.mult, op1=ALU.add))

            @block.tensor
            def _(pe):
                pe.wait_ge(s_rows, 7 * 16)
                split_of = lambda c: at_least(pe, s_slo, c)
                for step, i in steps:
                    if step == "chain":
                        n = turn_use[(step, i)]
                        at_least(pe, s_tlo, n - 3)
                        if i == 0:
                            split_of(4)
                        if i == 4:
                            split_of(6)
                            pe.wait_ge(s_tlo, turn_use[("chain", 3)] + 1)
                        a, b = (0, 0) if i < 4 else (2048, 2048)
                        m = i % 4
                        st = lambda y, k: y[:, a + k * D + m * P:a + k * D + (m + 1) * P]
                        mo = lambda y, k: y[:, b + k * D:b + (k + 1) * D]
                        passes(pe, turn_ps[n % 4][:], [(st(M_hi, k), st(M_lo, k), mo(Wq_hi, k), mo(Wq_lo, k))
                                                       for k in range(DC)]).then_inc(s_tp, 1)
                    if step == "turn":
                        n = turn_use[(step, i)]
                        at_least(pe, s_tlo, n - 3)
                        pe.wait_ge(s_cz, i + 1)
                        for k in range(DC):
                            tr = pe.transpose(turn_ps[n % 4][:, k * P:(k + 1) * P], ctx_n[:, k * P:(k + 1) * P], ident[:])
                        tr.then_inc(s_tp, 1)
                    if step == "kv":
                        if i == 0:
                            split_of(10)
                            pe.wait_ge(s_tlo, turn_use[("turn", 7)] + 1)
                        if i == 16:
                            split_of(14)
                        at_least(pe, s_kvo, i - 3)
                        w, p, half = (Wo_hi, Wo_lo) if i < 16 else (M_hi, M_lo), (i // 2) % 8, i % 2
                        st = lambda y, k: y[:, k * INNER + p * P:k * INNER + (p + 1) * P]
                        mo = lambda y, k: y[:, k * 1024 + half * BANK:k * 1024 + (half + 1) * BANK]
                        passes(pe, prod_ps[i % 4][:], [(st(w[0], k), st(w[1], k), mo(N_hi, k), mo(N_lo, k))
                                                       for k in range(DC)]).then_inc(s_kv, 1)

        two = lambda name: [sem(f"{name}{i}") for i in range(2)]
        s_xin = [sem(f"s_xin{i}") for i in range(RING)]
        s_xout = [sem(f"s_xout{i}") for i in range(RING)]
        s_kin, s_vin = sem("s_kin"), sem("s_vin")
        s_bn1, s_ag1, s_var1, s_rs1, s_xn = (sem(n) for n in ("s_bn1", "s_ag1", "s_var1", "s_rs1", "s_xn"))
        s_bn2, s_ag2, s_var2, s_rs2, s_x2n = (sem(n) for n in ("s_bn2", "s_ag2", "s_var2", "s_rs2", "s_x2n"))
        s_xT, s_xTh, s_xTl = sem("s_xT"), sem("s_xTh"), sem("s_xTl")
        s_x2T, s_x2Th, s_x2Tl = sem("s_x2T"), sem("s_x2Th"), sem("s_x2Tl")
        s_sc, s_sb, s_mx, s_sub, s_ex = two("s_sc"), two("s_sb"), two("s_mx"), two("s_sub"), two("s_ex")
        s_sum, s_inv, s_p = two("s_sum"), two("s_inv"), two("s_p")
        s_pT, s_pTh, s_pTl = two("s_pT"), two("s_pTh"), two("s_pTl")
        s_o, s_x2, s_f, s_fb, s_th, s_y = (sem(n) for n in ("s_o", "s_x2", "s_f", "s_fb", "s_th", "s_y"))
        s_m, s_mh, s_mr, s_mq, s_mlg, s_mlv = (sem(n) for n in ("s_m", "s_mh", "s_mr", "s_mq", "s_mlg", "s_mlv"))
        s_n, s_nh, s_nl = sem("s_n"), sem("s_nh"), sem("s_nl")
        s_bi, s_bs = two("s_bi"), sem("s_bs")
        s_ku, s_ks, s_kuh, s_kh, s_kp = (sem(n) for n in ("s_ku", "s_ks", "s_kuh", "s_kh", "s_kp"))
        s_kul = sem("s_kul")
        s_vh, s_vp = sem("s_vh"), sem("s_vp")

        heads = lambda a: a.rearrange("p (h j) -> p h j", j=CTX)
        half_of = lambda a, q: a[:, q * BANK:(q + 1) * BANK]
        H2 = H // 2

        def diag(part, half):
            blocks = bd[half * DH:(half + 1) * DH, :].rearrange("p (q c) -> p q c", c=2 * P)
            return blocks[:, :, part * P + half * CTX:part * P + (half + 1) * CTX]

        def bd_cols(p, part, n=1):
            return bd[:, (2 * p + part) * P:(2 * p + part + n) * P]

        def dense(y, half):
            return y[half * DH:(half + 1) * DH, :].rearrange("p (q j) -> p q j", j=CTX)

        def of_batch(y, b):
            return y[:, bass.ds(b * PAIRS, PAIRS)].unsqueeze(2).to_broadcast([P, PAIRS, CTX])

        def load_x(sp, u, r):
            at_least(sp, s_xout[r], 4 * (u - r) if not isinstance(u, int) else 16 * (u // RING))
            sp.dma_start(xr[r], x_t[bass.ds(u, 1), :, :].rearrange("o p d -> (o p) d")).then_inc(s_xin[r], 16)

        def x_loaded(eng, u, r):
            eng.wait_ge(s_xin[r], 4 * (u - r) + 16)

        def load_kv(sp, which, b, s):
            src = kv_scratch[which].rearrange("q p b j -> b p q j")[bass.ds(b, 1)].rearrange("o p q j -> (o p) q j")
            sp.dma_start(kvf.rearrange("p (q j) -> p q j", j=CTX), src).then_inc(s, 16)

        def load_k(sp, b):
            at_least(sp, s_vp, b)
            load_kv(sp, 0, b, s_kin)

        def load_v(sp, b):
            sp.wait_ge(s_kp, b + 1)
            load_kv(sp, 1, b, s_vin)

        def k_prepare_pool(pool, b):
            pool.wait_ge(s_kin, 16 * b + 16)
            q = lambda a: a.rearrange("p (q j) -> p q j", j=CTX)
            pool.tensor_tensor(q(kus), q(kvf), of_batch(U_fac, b), ALU.mult).then_inc(s_ku, 1)
            pool.wait_ge(s_ku, b + 1)
            pool.tensor_tensor(q(kvf), q(kvf), of_batch(F_fac, b), ALU.mult).then_inc(s_ks, 1)

        def ku_split_lo(pool, b):
            pool.wait_ge(s_kuh, b + 1)
            pool.tensor_tensor(ku_lo[:], kus, ku_hi[:].bitcast(F32), ALU.subtract).then_inc(s_kul, 1)

        def diag_lo(dve, s_hi, s_done, b):
            dve.wait_ge(s_hi, b + 1)
            for half in range(2):
                last = dve.tensor_tensor(diag(1, half), dense(kvf, half), diag(0, half).bitcast(F32), ALU.subtract)
            last.then_inc(s_done, 1)

        def k_prepare_act(act, b):
            at_least(act, s_bi[1], b)
            act.wait_ge(s_ku, b + 1)
            act.copy(ku_hi[:], kus).then_inc(s_kuh, 1)
            at_least(act, s_n, 8 * b)
            act.wait_ge(s_ks, b + 1)
            for half in range(2):
                last = act.copy(diag(0, half), dense(kvf, half))
            last.then_inc(s_kh, 1)

        def v_prepare_act(act, b):
            act.wait_ge(s_vin, 16 * b + 16)
            act.wait_ge(s_m, 16 * b + 16)
            for half in range(2):
                last = act.copy(diag(0, half), dense(kvf, half))
            last.then_inc(s_vh, 1)

        m_where = lambda c: ((c // 2) % 4, 2 * (c // 8) + c % 2)
        in_pairs = lambda a: a.rearrange("p (i n) -> p i n", i=2)

        def m_ps(c, s):
            return fold_ps[c % 4][:].rearrange("p (i s n) -> p i s n", i=2, s=2)[:, :, s, :]

        def m_part(y, c, dt=F32R):
            dc, g = m_where(c)
            col = dc * INNER + g * 2 * P
            return in_pairs(y[:, col:col + 2 * P].bitcast(dt))

        def m_bank_read(pe, b8, c):
            if c % 2:
                pe.wait_ge(s_mlv, b8 + c // 2 + 1)
            else:
                pe.wait_ge(s_mr, 2 * b8 + c + 1)
                pe.wait_ge(s_mq, b8 + c // 2 + 1)

        def fold_m_pe(pe, b8, cs, free=lambda c: None):
            for c in cs:
                if c == 0:
                    pe.wait_ge(s_kp, b8 // 8 + 1)
                if c < 4:
                    free(c)
                else:
                    m_bank_read(pe, b8, c - 4)
                dc, g = m_where(c)
                for i in range(2):
                    p = 2 * g + i
                    st = lambda y: y[:, p * D + dc * P:p * D + (dc + 1) * P]
                    ps = fold_ps[c % 4][:, i * 2 * P:(i + 1) * 2 * P]
                    pe.matmul(ps, st(Wq_hi), bd_cols(p, 0, 2), start=True, stop=False)
                    mm = pe.matmul(ps[:, 0:P], st(Wq_lo), bd_cols(p, 0), start=False, stop=True)
                mm.then_inc(s_m, 1)

        def bias_pe(pe, b8):
            pe.wait_ge(s_kul, b8 // 8 + 1)
            for half in range(2):
                pe.matmul(bias_ps[half][:], half_ones[half][:], ku_hi[:], start=True, stop=False)
                pe.matmul(bias_ps[half][:], half_ones[half][:], ku_lo[:], start=False, stop=True).then_inc(s_bi[half], 1)

        def m_act(act, b8, cs):
            for c in cs:
                act.wait_ge(s_m, 2 * b8 + c + 1)
                if c % 2 == 0:
                    k = c // 2
                    if k >= 2:
                        act.wait_ge(s_mlg, b8 + k - 1)
                    act.copy(in_pairs(m_cross[k % 2]), m_ps(c, 1)).then_inc(s_mq, 1)
                act.copy(m_part(M_hi, c), m_ps(c, 0)).then_inc(s_mh, 1)

        def m_dve(dve, b8, cs):
            for c in cs:
                k = c // 2
                rest = in_pairs((m_rest_v if c % 2 else m_rest_g)[k % 2])
                if c == 1:
                    dve.wait_ge(s_kul, b8 // 8 + 1)
                if k >= 2:
                    dve.wait_ge(s_mlv if c % 2 else s_mlg, b8 + k - 1)
                dve.wait_ge(s_mh, 2 * b8 + c + 1)
                dve.tensor_tensor(rest, m_ps(c, 0), m_part(M_hi, c, F32), ALU.subtract).then_inc(s_mr, 1)
                if c % 2:
                    dve.wait_ge(s_mr, 2 * b8 + c + 1)
                    dve.tensor_tensor(m_part(M_lo, c), m_ps(c, 1), rest, ALU.add).then_inc(s_mlv, 1)

        def m_pool(pool, b8, ks):
            for k in ks:
                pool.wait_ge(s_mr, 2 * b8 + 2 * k + 1)
                pool.wait_ge(s_mq, b8 + k + 1)
                pool.tensor_tensor(m_part(M_lo, 2 * k), in_pairs(m_rest_g[k % 2]), in_pairs(m_cross[k % 2]),
                                   ALU.add).then_inc(s_mlg, 1)

        def fold_n_pe(pe, b8, free):
            pe.wait_ge(s_vp, b8 // 8 + 1)
            for p in range(PAIRS):
                if p < 4:
                    free(p)
                else:
                    pe.wait_ge(s_nl, b8 + p - 3)
                mo = lambda y: y[:, p * D:(p + 1) * D]
                passes(pe, fold_ps[p % 4][:], [(bd_cols(p, 0), bd_cols(p, 1), mo(Wo_hi), mo(Wo_lo))]).then_inc(s_n, 1)

        def fold_hi(act, b8, produced, done, dst):
            for c in range(8):
                act.wait_ge(produced, b8 + c + 1)
                act.copy(dst(c), fold_ps[c % 4][:]).then_inc(done, 1)

        def fold_lo(dve, b8, produced, done, hi, lo):
            for c in range(8):
                dve.wait_ge(produced, b8 + c + 1)
                dve.tensor_tensor(lo(c), fold_ps[c % 4][:], hi(c).bitcast(F32), ALU.subtract).then_inc(done, 1)

        def bias_copy(dve, b8):
            for half in range(2):
                dve.wait_ge(s_bi[half], b8 // 8 + 1)
                last = dve.tensor_copy(bias.rearrange("p (q s j) -> p q s j", s=2, j=CTX)[:, :, half, :],
                                       bias_ps[half][:].rearrange("p (q j) -> p q j", j=CTX))
            last.then_inc(s_bs, 1)

        n_cols = lambda y, c: y[:, c * D:(c + 1) * D]
        N_fold = (s_nh, s_nl, lambda c: n_cols(N_hi, c), lambda c: n_cols(N_lo, c))

        def layernorm_stats(dve, src, bn, mv, var, s_bn_, s_ag_, s_var_, u, mul, add, between=None):
            dve.bn_stats(bn[:], src).then_inc(s_bn_, 1)
            dve.wait_ge(s_bn_, u + 1)
            if between:
                between()
            dve.bn_aggr(mv[:], bn[:]).then_inc(s_ag_, 1)
            dve.wait_ge(s_ag_, u + 1)
            dve.tensor_scalar(var[:], mv[:, 1:2], mul, add, ALU.mult, ALU.add).then_inc(s_var_, 1)

        def turn(pe, ps, src, s):
            for k in range(4):
                tr = pe.transpose(ps[:, k * P:(k + 1) * P], src[:, k * P:(k + 1) * P], ident[:])
            tr.then_inc(s, 1)

        def ln1_stats(dve, u, r, between=None):
            x_loaded(dve, u, r)
            layernorm_stats(dve, xr[r], bn1, mv1, var1, s_bn1, s_ag1, s_var1, u, 1.0 + EPS,
                            EPS * EPS, between)

        def ln1_apply(dve, u, r):
            dve.wait_ge(s_rs1, u + 1)
            at_least(dve, s_xT, u)
            dve.tensor_scalar(xn, xr[r], mv1[:, 0:1], rs1[:, 0:1], ALU.subtract, ALU.mult).then_inc(s_xn, 1)

        def pow1(pool, u):
            pool.wait_ge(s_var1, u + 1)
            at_least(pool, s_xn, u)
            pool.tensor_tensor(rs1[:], var1[:], minus_half[:], ALU.pow).then_inc(s_rs1, 1)

        def turn_xn(pe, u):
            pe.wait_ge(s_xn, u + 1)
            turn(pe, xT_ps, xn, s_xT)

        def xT_split_hi(act, u):
            act.wait_ge(s_xT, u + 1)
            at_least(act, s_sc[1], u)
            act.copy(xT_hi[:], xT_ps[:]).then_inc(s_xTh, 1)

        def xT_split_lo(dve, u):
            dve.wait_ge(s_xTh, u + 1)
            at_least(dve, s_sc[1], u)
            dve.tensor_tensor(xT_lo[:], xT_ps[:], xT_hi[:].bitcast(F32), ALU.subtract).then_inc(s_xTl, 1)

        def parts(t, m, first):
            known = isinstance(t, int)
            return dict(scores=not known or t < T, following=not known or t + 1 < T,
                        attn=not known or 1 <= t <= T, chain=not known or t >= 2,
                        fold_m=m == 7 and (not known or t + 1 < T), fold_n=m == 0 and (not known or 0 < t < T),
                        more=not known or t + TPB < T)

        def slot_sp(sp, t, m):
            has = parts(t, m, False)
            if has["more"] and m == 2:
                load_k(sp, (t + 6) // 8)
            if has["chain"]:
                sp.wait_ge(s_y, t - 1)
                r = (m - 2) % RING
                sp.dma_start(out_t[bass.ds(t - 2, 1), :, :].rearrange("o p d -> (o p) d"), xr[r]).then_inc(s_xout[r], 16)
            if not isinstance(t, int) or t + 2 < T:
                load_x(sp, t + 2, (m + 2) % RING)
            if has["more"] and m == 5:
                load_v(sp, (t + 3) // 8)

        def slot_pe(pe, t, m):
            has = parts(t, m, False)
            if has["scores"]:
                pe.wait_ge(s_xTh, t + 1)
                for q in range(2):
                    if m == 0:
                        pe.wait_ge(s_mlg, t + 4 * q + 4)
                        pe.wait_ge(s_mlv, t + 4 * q + 4)
                        m_bank_read(pe, t, 12 + q)
                    if m == 1:
                        pe.wait_ge(s_nl, t + 4 + q)
                    at_least(pe, s_sb[q], t)
                    mo = lambda y, k: y[:, k * INNER + q * BANK:k * INNER + (q + 1) * BANK]
                    st = lambda y, k: y[:, k * P:(k + 1) * P]
                    passes(pe, S_ps[q][:], [(st(xT_hi, k), st(xT_lo, k), mo(M_hi, k), mo(M_lo, k)) for k in range(DC)],
                           (lambda: pe.wait_ge(s_xTl, t + 1)) if q == 0 else None).then_inc(s_sc[q], 1)
            if has["chain"]:
                pe.wait_ge(s_x2n, t - 1)
                at_least(pe, s_x2Tl, t - 2)
                turn(pe, x2T_ps, x2n, s_x2T)
            if has["fold_m"]:
                pe.wait_ge(s_x2, t - 1)
                bias_pe(pe, t + 1)
            if has["attn"]:
                if m == 1:
                    pe.wait_ge(s_nl, t + 7)
                for q in range(2):
                    pe.wait_ge(s_p[q], t)
                    at_least(pe, s_pTl[q], t - 1)
                    turn(pe, pT_ps[q], half_of(S[(m - 1) % 2], q), s_pT[q])
            if has["chain"]:
                pe.wait_ge(s_x2Th, t - 1)
                at_least(pe, s_fb, t - 2)
                st = lambda y, k: y[:, k * P:(k + 1) * P]
                mo = lambda y, k: y[:, k * D:(k + 1) * D]

                def before_lo():
                    if has["fold_m"]:
                        fold_m_pe(pe, t + 1, (0, 1), lambda c: pe.wait_ge(s_sb[c], t + 1))
                    pe.wait_ge(s_x2Tl, t - 1)
                passes(pe, F_ps[:], [(st(x2T_hi, k), st(x2T_lo, k), mo(W3_hi, k), mo(W3_lo, k)) for k in range(DC)],
                       before_lo).then_inc(s_f, 1)
            if has["attn"]:
                at_least(pe, s_x2, t - 1)
            for quarter in range(4):
                if has["fold_m"]:
                    fold_m_pe(pe, t + 1, ((2, 3, 4), (5, 6, 7), (8, 9, 10, 11), (12, 13, 14, 15))[quarter],
                              lambda c: pe.wait_ge(s_pTl[c - 2], t))
                    if quarter == 0:
                        pe.wait_ge(s_bs, t // 8 + 1)
                if has["attn"]:
                    q, ks = quarter // 2, (2 * quarter, 2 * quarter + 1)
                    pe.wait_ge(s_pTh[q], t)
                    for k in ks:
                        for mv in (N_hi, N_lo):
                            pe.matmul(O_ps[:], pT_hi[:, k * P:(k + 1) * P], n_cols(mv, k),
                                      start=(k == 0 and mv is N_hi), stop=False)
                    pe.wait_ge(s_pTl[q], t)
                    for k in ks:
                        mm = pe.matmul(O_ps[:], pT_lo[:, k * P:(k + 1) * P], n_cols(N_hi, k), start=False, stop=(k == 7))
                    if quarter == 3:
                        mm.then_inc(s_o, 1)
                if quarter == (2 if has["fold_m"] else 1) and has["following"]:
                    turn_xn(pe, t + 1)
            if has["fold_n"]:
                fold_n_pe(pe, t, lambda c: pe.wait_ge(s_sb[c], t + 1) if c < 2 else None)

        def slot_act(act, t, m):
            has = parts(t, m, False)

            def exp(q):
                act.wait_ge(s_sub[q], t + 1)
                s = half_of(S[m % 2], q)
                act.activation(s, s, ACT.Exp).then_inc(s_ex[q], 1)

            if has["chain"]:
                act.wait_ge(s_x2T, t - 1)
                at_least(act, s_f, t - 2)
                act.copy(x2T_hi[:], x2T_ps[:]).then_inc(s_x2Th, 1)
            if has["attn"]:
                at_least(act, s_o, t - 1)
                for q in range(2):
                    act.wait_ge(s_pT[q], t)
                    act.copy(half_of(pT_hi, q), pT_ps[q][:]).then_inc(s_pTh[q], 1)
            if has["scores"]:
                exp(0)
                exp(1)
            if has["fold_n"]:
                v_prepare_act(act, t // 8)
            if has["more"] and m == 4:
                k_prepare_act(act, (t + 4) // 8)
            if has["fold_m"]:
                m_act(act, t + 1, range(10))
            if has["chain"]:
                act.wait_ge(s_fb, t - 1)
                act.activation(hid, hid, ACT.Tanh).then_inc(s_th, 1)
            if has["fold_m"]:
                m_act(act, t + 1, range(10, 12))
            if has["following"]:
                xT_split_hi(act, t + 1)
            if has["fold_m"]:
                m_act(act, t + 1, range(12, 16))
            if has["fold_n"]:
                fold_hi(act, t, s_n, s_nh, N_fold[2])

        def slot_dve(dve, t, m):
            has = parts(t, m, False)
            r2 = (m - 2) % RING

            def read_scores(q):
                dve.wait_ge(s_sc[q], t + 1)
                at_least(dve, s_pT[q], t - 1)
                if m == 0 and q == 0:
                    dve.wait_ge(s_bs, t // 8 + 1)
                    dve.wait_ge(s_mlg, t + 8)
                dve.tensor_tensor(half_of(S[m % 2], q), S_ps[q][:], half_of(bias, q), ALU.add).then_inc(s_sb[q], 1)

            def maximum(q):
                dve.wait_ge(s_sb[q], t + 1)
                dve.tensor_reduce(row_max[m % 2][:, q * H2:(q + 1) * H2], heads(half_of(S[m % 2], q)), AX_X,
                                  ALU.max).then_inc(s_mx[q], 1)

            if has["chain"]:
                dve.wait_ge(s_o, t - 1)
                dve.tensor_tensor(xr[r2], O_ps[:], xr[r2], ALU.add).then_inc(s_x2, 1)
                dve.wait_ge(s_x2, t - 1)
                layernorm_stats(dve, xr[r2], bn2, mv2, var2, s_bn2, s_ag2, s_var2, t - 2, 1.0, EPS,
                                (lambda: read_scores(0)) if has["scores"] else None)
            elif has["scores"]:
                read_scores(0)
            if has["scores"]:
                maximum(0)
            if has["chain"]:
                dve.wait_ge(s_rs2, t - 1)
                at_least(dve, s_x2T, t - 2)
                dve.tensor_scalar(x2n, xr[r2], mv2[:, 0:1], rs2[:, 0:1], ALU.subtract, ALU.mult).then_inc(s_x2n, 1)
            if has["following"]:
                ln1_stats(dve, t + 1, (m + 1) % RING, lambda: read_scores(1))
            elif has["scores"]:
                read_scores(1)
            if has["chain"]:
                dve.wait_ge(s_x2Th, t - 1)
                at_least(dve, s_f, t - 2)
                dve.tensor_tensor(x2T_lo[:], x2T_ps[:], x2T_hi[:].bitcast(F32), ALU.subtract).then_inc(s_x2Tl, 1)
            if has["scores"]:
                maximum(1)
            if has["following"]:
                ln1_apply(dve, t + 1, (m + 1) % RING)
            if has["attn"]:
                at_least(dve, s_o, t - 1)
                for q in range(2):
                    dve.wait_ge(s_pTh[q], t)
                    dve.tensor_tensor(half_of(pT_lo, q), pT_ps[q][:], half_of(pT_hi, q).bitcast(F32),
                                      ALU.subtract).then_inc(s_pTl[q], 1)
            if has["fold_n"]:
                diag_lo(dve, s_vh, s_vp, t // 8)
            if has["fold_m"]:
                bias_copy(dve, t + 1)
                m_dve(dve, t + 1, range(2))
            if has["scores"]:
                for q in range(2):
                    hs = slice(q * H2, (q + 1) * H2)
                    dve.wait_ge(s_ex[q], t + 1)
                    dve.tensor_reduce(row_sum[m % 2][:, hs], heads(half_of(S[m % 2], q)), AX_X, ALU.add).then_inc(s_sum[q], 1)
                    if has["fold_m"]:
                        m_dve(dve, t + 1, range(2 + 2 * q, 4 + 2 * q))
                    dve.wait_ge(s_sum[q], t + 1)
                    dve.reciprocal(row_inv[m % 2][:, hs], row_sum[m % 2][:, hs]).then_inc(s_inv[q], 1)
            if has["chain"]:
                dve.wait_ge(s_f, t - 1)
                at_least(dve, s_y, t - 2)
                dve.tensor_tensor(hid, F_ps[:], ffn_bias_row[:], ALU.add).then_inc(s_fb, 1)
            if has["more"] and m == 4:
                diag_lo(dve, s_kh, s_kp, (t + 4) // 8)
            if has["fold_m"]:
                m_dve(dve, t + 1, range(6, 12))
            if has["following"]:
                xT_split_lo(dve, t + 1)
            if has["fold_m"]:
                m_dve(dve, t + 1, range(12, 16))
            if has["fold_n"]:
                fold_lo(dve, t, *N_fold)

        def slot_pool(pool, t, m):
            has = parts(t, m, False)

            def by_head(q, row, op, s_wait, s_done):
                s = heads(half_of(S[m % 2], q))
                pool.wait_ge(s_wait[q], t + 1)
                pool.tensor_tensor(s, s, row[m % 2][:, q * H2:(q + 1) * H2].unsqueeze(2).to_broadcast([P, H2, CTX]),
                                   op).then_inc(s_done[q], 1)

            if has["chain"]:
                pool.wait_ge(s_var2, t - 1)
                at_least(pool, s_x2n, t - 2)
                pool.tensor_tensor(rs2[:], var2[:], minus_half[:], ALU.pow).then_inc(s_rs2, 1)
            if has["scores"]:
                by_head(0, row_max, ALU.subtract, s_mx, s_sub)
            if has["following"]:
                pow1(pool, t + 1)
            if has["scores"]:
                by_head(1, row_max, ALU.subtract, s_mx, s_sub)
            if has["fold_m"]:
                m_pool(pool, t + 1, range(1))
            if has["scores"]:
                by_head(0, row_inv, ALU.mult, s_inv, s_p)
            if has["fold_m"]:
                m_pool(pool, t + 1, range(1, 3))
            if has["scores"]:
                by_head(1, row_inv, ALU.mult, s_inv, s_p)
            if has["chain"]:
                if has["fold_m"]:
                    m_pool(pool, t + 1, range(3, 5))
                r2 = (m - 2) % RING
                pool.wait_ge(s_th, t - 1)
                pool.tensor_tensor(xr[r2], xr[r2], hid, ALU.add).then_inc(s_y, 1)
            if has["fold_m"]:
                m_pool(pool, t + 1, range(5, 8))
            if has["more"] and m == 3:
                k_prepare_pool(pool, (t + 5) // 8)
            if has["more"] and m == 4:
                ku_split_lo(pool, (t + 4) // 8)

        def run(eng, slot):
            for t in range(2):
                slot(eng, t, t)
            with eng.Fori(0, B - 1) as b:
                for j in range(2, TPB + 2):
                    slot(eng, b * TPB + j, j % TPB)
            for t in range(T - 6, T + 2):
                slot(eng, t, t % TPB)

        with nc.Block() as block:
            @block.sync
            def _(sp):
                load_x(sp, 0, 0)
                load_k(sp, 0)
                load_x(sp, 1, 1)
                load_v(sp, 0)
                run(sp, slot_sp)
                for r in range(RING):
                    sp.wait_ge(s_xout[r], 16 * (T // RING))

            @block.tensor
            def _(pe):
                turn_xn(pe, 0)
                fold_m_pe(pe, 0, range(16))
                pe.wait_ge(s_xTl, 1)
                bias_pe(pe, 0)
                fold_n_pe(pe, 0, lambda c: m_bank_read(pe, 0, 12 + c))
                pe.wait_ge(s_nl, 8)
                run(pe, slot_pe)

            @block.scalar
            def _(act):
                k_prepare_act(act, 0)
                xT_split_hi(act, 0)
                m_act(act, 0, range(16))
                v_prepare_act(act, 0)
                fold_hi(act, 0, s_n, s_nh, N_fold[2])
                run(act, slot_act)

            @block.vector
            def _(dve):
                ln1_stats(dve, 0, 0)
                ln1_apply(dve, 0, 0)
                diag_lo(dve, s_kh, s_kp, 0)
                xT_split_lo(dve, 0)
                m_dve(dve, 0, range(16))
                bias_copy(dve, 0)
                diag_lo(dve, s_vh, s_vp, 0)
                fold_lo(dve, 0, *N_fold)
                run(dve, slot_dve)

            @block.gpsimd
            def _(pool):
                pow1(pool, 0)
                k_prepare_pool(pool, 0)
                ku_split_lo(pool, 0)
                m_pool(pool, 0, range(8))
                run(pool, slot_pool)


def kernel(x, ctx_1024, fside_Bx16_0, L0_xattn_ln1_w, L0_xattn_ln1_b, L0_xattn_ln2_w, L0_xattn_ln2_b,
           L0_xattn_Wq, L0_xattn_Wkv, L0_xattn_Wout, L0_ffn_weight, L0_ffn_aux_weight1, L0_ffn_aux_weight2,
           L0_ffn_bias):
    import concourse.bacc as bacc
    from concourse.bass_utils import run_bass_kernel_spmd

    fs_cols = np.ascontiguousarray(
        np.repeat(np.asarray(fside_Bx16_0).reshape(B, PAIRS, 2).transpose(2, 0, 1).reshape(2, 1, B * PAIRS), P // 2, axis=1)
        .reshape(P, B * PAIRS))
    arrays = {
        "x": np.ascontiguousarray(x),
        "ctx_rows": np.ascontiguousarray(np.asarray(ctx_1024).reshape(B * CTX, D)),
        "fs_cols": fs_cols,
        "ln1_w": np.ascontiguousarray(L0_xattn_ln1_w), "ln1_b": np.ascontiguousarray(L0_xattn_ln1_b),
        "ln2_w": np.ascontiguousarray(L0_xattn_ln2_w), "ln2_b": np.ascontiguousarray(L0_xattn_ln2_b),
        "wqT": np.ascontiguousarray(np.asarray(L0_xattn_Wq).T),
        "wkv": np.ascontiguousarray(L0_xattn_Wkv), "wout": np.ascontiguousarray(L0_xattn_Wout),
        "ffn_wT": np.ascontiguousarray(np.asarray(L0_ffn_weight).T),
        "aux1T": np.ascontiguousarray(np.asarray(L0_ffn_aux_weight1).T),
        "aux2": np.ascontiguousarray(L0_ffn_aux_weight2),
        "ffn_bias": np.ascontiguousarray(L0_ffn_bias),
        "ident_in": np.eye(P, dtype=np.float32),
    }
    nc = bacc.Bacc("TRN2", target_bir_lowering=False, num_devices=1)
    args = [nc.dram_tensor(f"{name}_dram", a.shape, mybir.dt.from_np(a.dtype), kind="ExternalInput").ap()
            for name, a in arrays.items()]
    out = nc.dram_tensor("y_dram", (B, ROWS, D), F32, kind="ExternalOutput").ap()
    build(nc, *args, out)
    r = run_bass_kernel_spmd(nc, [{f"{name}_dram": a for name, a in arrays.items()}], core_ids=[0])
    return r.results[0]["y_dram"]
```

```python
from contextlib import ExitStack

import numpy as np

import concourse.bass as bass
from concourse import mybir

F32 = mybir.dt.float32
F32R = mybir.dt.float32r
ALU = mybir.AluOpType
ACT = mybir.ActivationFunctionType
AX_X = mybir.AxisListType.X

P = 128
BANK = 512
EPS = 1e-5
B, ROWS, D = 16, 1024, 512
CTX, H, DH = 64, 16, 64
INNER = H * DH
PAIRS = H // 2
DC = D // P
TPB = ROWS // P
T = B * TPB
RING = 4
SCALE = DH ** -0.5
assert DH == CTX == P // 2 and D == BANK and INNER == 2 * BANK and TPB == 8 and TPB % RING == 0


def build(nc, x, x_turned, ctx_rows, fs_cols, ln1_w, ln1_b, ln2_w, ln2_b, wqT, wkv, wout, ffn_wT, aux1T, aux2,
          ffn_bias, ident_in, out):
    kv_scratch = nc.dram_tensor("kv_scratch", (2, PAIRS, P, B, CTX), F32, kind="Internal").ap()
    x_t = x.rearrange("b (n p) d -> (b n) p d", p=P)
    xT_t = x_turned
    out_t = out.rearrange("b (n p) d -> (b n) p d", p=P)

    with ExitStack() as ctx:
        def sb(name, cols, dt=F32):
            return ctx.enter_context(nc.sbuf_tensor(name, [P, cols], dt))

        def sem(name):
            return ctx.enter_context(nc.semaphore(name))

        M_hi, M_lo = sb("M_hi", DC * INNER, F32R), sb("M_lo", DC * INNER, F32R)
        N_hi, N_lo = sb("N_hi", PAIRS * D, F32R), sb("N_lo", PAIRS * D, F32R)
        Wq_hi, Wq_lo = sb("Wq_hi", PAIRS * D, F32R), sb("Wq_lo", PAIRS * D, F32R)
        Wo_hi, Wo_lo = sb("Wo_hi", PAIRS * D, F32R), sb("Wo_lo", PAIRS * D, F32R)
        W3_hi, W3_lo = sb("W3_hi", DC * D, F32R), sb("W3_lo", DC * D, F32R)
        bd = sb("bd", PAIRS * 2 * P, F32R)
        ku_hi, ku_lo = sb("ku_hi", PAIRS * CTX, F32R), sb("ku_lo", PAIRS * CTX, F32R)
        xT_hi, xT_lo = sb("xT_hi", D, F32R), sb("xT_lo", D, F32R)
        x2T_hi, x2T_lo = sb("x2T_hi", D, F32R), sb("x2T_lo", D, F32R)
        with nc.sbuf_tensor("stage_more", [P, 4 * D], F32) as stage_more:
            pass
        pT_hi, pT_lo = sb("pT_hi", INNER, F32R), sb("pT_lo", INNER, F32R)
        half_ones = [sb(f"half_ones{i}", P, F32R) for i in range(2)]
        ident = sb("ident", P)
        ffn_bias_row = sb("ffn_bias_row", D)
        fs = sb("fs", B * PAIRS)
        F_fac = sb("F_fac", B * PAIRS)
        U_fac = sb("U_fac", B * PAIRS)
        bq = sb("bq", PAIRS)
        minus_half = sb("minus_half", 1)
        zero_col = sb("zero_col", 1)
        bn1, bn2, bn_w = sb("bn1", 6), sb("bn2", 6), sb("bn_w", 6)
        mv1, mv2, mv_w = sb("mv1", 2), sb("mv2", 2), sb("mv_w", 8)
        var1, var2 = sb("var1", 1), sb("var2", 1)
        rs1, rs2 = sb("rs1", 1), sb("rs2", 1)
        row_max = [sb(f"row_max{i}", H) for i in range(2)]
        row_sum = [sb(f"row_sum{i}", H) for i in range(2)]
        row_inv = [sb(f"row_inv{i}", H) for i in range(2)]

        area = sb("area", 15 * D)

        def carve():
            at = [0]

            def take(cols):
                at[0] += cols
                assert at[0] <= 15 * D
                return area[:, at[0] - cols:at[0]]
            return take

        take = carve()
        stage = [take(2 * D) for _ in range(3)]
        ctx_in = [take(D) for _ in range(3)]
        kv_out = [take(D) for _ in range(2)]
        ln1_w_row, ln1_b_row, ln2_w_row, ln2_b_row = (take(D) for _ in range(4))
        take = carve()
        xr = [take(D) for _ in range(RING)]
        S = [take(INNER) for _ in range(2)]
        xT = [take(D) for _ in range(2)]
        hid = take(D)
        bias = take(INNER)
        kvf, kus = take(PAIRS * CTX), take(PAIRS * CTX)
        m_rest_v, m_cross, m_rest_g = ([y[:, i * 2 * P:(i + 1) * 2 * P] for i in range(2)]
                                       for y in (kus, S[0][:, 0:BANK], S[0][:, BANK:INNER]))

        banks = [ctx.enter_context(nc.psum_tensor(f"bank{i}", [P, BANK], F32)) for i in range(8)]
        S_ps, pT_ps = banks[0:2], banks[2:4]
        spare_ps, x2T_ps, O_ps, F_ps = banks[4:8]
        fold_ps = S_ps + pT_ps
        bias_ps = (O_ps, spare_ps)

        def at_least(eng, s, n):
            if not isinstance(n, int) or n > 0:
                eng.wait_ge(s, n)

        def passes(eng, ps, pairs, wait_lo=None, last=True):
            n = 0
            for sh, _, mh, ml in pairs:
                for mv in (mh, ml):
                    mm = eng.matmul(ps, sh, mv, start=(n == 0), stop=False)
                    n += 1
            if wait_lo:
                wait_lo()
            for k, (_, sl, mh, _) in enumerate(pairs):
                mm = eng.matmul(ps, sl, mh, start=False, stop=(k == len(pairs) - 1))
            return mm

        RING_W = 5
        stage = stage + [stage_more[:, i * 2 * D:(i + 1) * 2 * D] for i in range(2)]
        wk_v = wkv.rearrange("(k p) (s n) -> s k p n", p=P, s=2)
        pairs_of = lambda w: w.rearrange("(g k p) n -> g p k n", p=P, k=2)
        A1, A2, W = pairs_of(aux1T), pairs_of(aux2), pairs_of(ffn_wT)
        WQ, WO = pairs_of(wqT), pairs_of(wout)
        chunks = []
        for g in range(2):
            chunks += [(A1[g], M_hi, M_lo, g * 1024, None), (A2[g], Wq_hi, Wq_lo, g * 1024, None)]
        chunks += [(W[g], M_hi, M_lo, 2048 + g * 1024, None) for g in range(2)]
        chunks += [(wk_v[0, k], Wo_hi, Wo_lo, k * 1024, None) for k in range(4)]
        WV_FIRST = len(chunks)
        chunks += [(wk_v[1, k], M_hi, M_lo, k * 1024, "w3") for k in range(4)]
        WQ_FIRST = len(chunks)
        chunks += [(WQ[g], Wq_hi, Wq_lo, g * 1024, "w3") for g in range(4)]
        chunks += [(WO[g], Wo_hi, Wo_lo, g * 1024, "k") for g in range(4)]
        CHUNKS = len(chunks)
        turn_bank, prod_ps = banks[0:4], banks[4:8]
        CTX_TILES = B * CTX // P

        pe_steps = [("mix", 0), ("mix", 1), ("turn", 0), ("w3", 0), ("w3", 1), ("turn", 1),
                    ("w3", 2), ("turn", 2), ("w3", 3), ("turn", 3)]
        steps = [("split", 0), ("split", 1), ("stats", 0), ("norm", 0), ("split", 2), ("split", 3),
                 ("center", 4), ("center", 5), ("split", 4), ("a12", 0), ("a12", 1), ("split", 5),
                 ("a12", 2), ("a12", 3), ("turn", 0), ("load", 3), ("stats", 1), ("norm", 1), ("split", 6),
                 ("stats", 2), ("norm", 2), ("w3", 0), ("split", 7), ("w3", 1), ("turn", 1), ("load", 4),
                 ("stats", 3), ("norm", 3), ("split", 8), ("w3", 2), ("turn", 2), ("load", 5), ("split", 9),
                 ("w3", 3), ("turn", 3), ("load", 6), ("stats", 4), ("norm", 4)]
        beside = {0: [("split", 10), ("stats", 5), ("norm", 5)], 1: [("split", 11)],
                  2: [("turn", 4), ("load", 7), ("stats", 6), ("norm", 6)], 3: [("split", 12)],
                  4: [("turn", 5), ("stats", 7), ("norm", 7)], 5: [("split", 13)], 6: [("turn", 6)], 8: [("turn", 7)],
                  18: [("factors", 0)], 21: [("k0", 0)], 29: [("x0", 0)]}
        for g in range(4):
            beside[(9, 10, 12, 14)[g]] = [("fold", g), ("center", WQ_FIRST + g)]
            beside[11 + 2 * g] = [("split", WQ_FIRST + g)]
            beside[25 + g] = [("split", WQ_FIRST + 4 + g)]
        for n in range(4 * PAIRS):
            pe_steps += [("kv", n)] + ([("turn", 4 + n // 2)] if n in (1, 3, 5, 7) else [])
            steps += [("kv", n)] + beside.get(n, [])
        kv_where = lambda n: ((n // 8) % 2, n // 16, n % 8)

        s_const, s_ones, s_ident, s_ln1, s_rows = (sem(n) for n in ("s_const", "s_ones", "s_ident", "s_ln1", "s_rows"))
        s_stage = [sem(f"s_stage{i}") for i in range(RING_W)]
        s_ctx = [sem(f"s_ctx{i}") for i in range(3)]
        CENTERED = {c: n for n, c in enumerate((4, 5, *range(WQ_FIRST, WQ_FIRST + 4)))}
        s_wbn, s_wag, s_wc = sem("s_wbn"), sem("s_wag"), sem("s_wc")
        s_bq, s_fold, s_fac = sem("s_bq"), sem("s_fold"), sem("s_fac")
        s_shi, s_slo = sem("s_shi"), sem("s_slo")
        s_cbn, s_cag, s_cv, s_crs, s_cz, s_czw, s_czb = (sem(n) for n in (
            "s_cbn", "s_cag", "s_cv", "s_crs", "s_cz", "s_czw", "s_czb"))
        s_a12, s_w3, s_turn = ([sem(f"{n}{w}") for w in ("", "_hi", "_lo")] for n in ("s_a12", "s_w3", "s_turn"))
        s_kv, s_kvo = sem("s_kv"), sem("s_kvo")
        s_kvst = [sem(f"s_kvst{i}") for i in range(2)]

        def evacuated(step, i):
            if step == "turn":
                cut = lambda y: y.rearrange("p (k r) -> p k r", k=DC)
                return [cut(y[:, :])[:, :, i * P:(i + 1) * P] for y in (N_hi, N_lo)] + [cut(turn_bank[i % 4][:])]
            hi, lo, col = (Wq_hi, Wq_lo, 2048) if step == "a12" else (W3_hi, W3_lo, 0)
            return [y[:, col + i * D:col + (i + 1) * D] for y in (hi, lo)] + [prod_ps[i][:]]

        sems_of = {"a12": s_a12, "w3": s_w3, "turn": s_turn}

        ctx_t = ctx_rows.rearrange("(n p) d -> n p d", p=P)

        def setup_sp(sp):
            def load_chunk(c):
                at_least(sp, s_slo, c - RING_W + 1)
                dst, src = stage[c % RING_W], chunks[c][0]
                if len(src.shape) == 3:
                    dst = dst.rearrange("p (k n) -> p k n", k=2)
                sp.dma_start(dst, src).then_inc(s_stage[c % RING_W], 16)

            def load_row(row, dst, s):
                sp.dma_start(dst, row.rearrange("(a n) -> a n", a=1).to_broadcast([P, D])).then_inc(s, 16)

            def load_ctx(i):
                sp.dma_start(ctx_in[i % 3], ctx_t[i]).then_inc(s_ctx[i % 3], 16)

            load_chunk(0)
            load_chunk(1)
            load_ctx(0)
            load_chunk(2)
            load_row(ln1_w, ln1_w_row, s_ln1)
            load_row(ln1_b, ln1_b_row, s_ln1)
            load_chunk(3)
            load_ctx(1)
            sp.dma_start(ident[:], ident_in).then_inc(s_ident, 16)
            load_chunk(4)
            for step, i in steps:
                if step == "split" and i + RING_W < CHUNKS:
                    load_chunk(i + RING_W)
                if step == "load":
                    sp.wait_ge(s_turn[0], i - 2)
                    load_ctx(i)
                if step == "split" and i == 0:
                    load_ctx(2)
                if step == "w3" and i == 0:
                    load_row(ln2_w, ln2_w_row, s_rows)
                    load_row(ln2_b, ln2_b_row, s_rows)
                    load_row(ffn_bias, ffn_bias_row[:], s_rows)
                    sp.dma_start(fs[:], fs_cols).then_inc(s_rows, 16)
                if step == "kv":
                    which, half, p = kv_where(i)
                    sp.wait_ge(s_kvo, i + 1)
                    sp.dma_start(kv_scratch[which, p, :, half * 8:half * 8 + 8, :],
                                 kv_out[i % 2].rearrange("p (b j) -> p b j", b=8)).then_inc(s_kvst[i % 2], 16)
                if step == "k0":
                    for q in s_kvst:
                        sp.wait_ge(q, 16 * 4)
                    sp.wait_ge(s_fold, 4)
                    load_k(sp, 0)
                if step == "x0":
                    sp.wait_ge(s_slo, CHUNKS)
                    load_x(sp, 0, 0)
                    load_x(sp, 1, 1)
                    sp.wait_ge(s_bq, 2 * 4)
                    load_xT(sp, 0, 0)
            for q in s_kvst:
                sp.wait_ge(q, 16 * 16)
            load_xT(sp, 1, 1)
            load_v(sp, 0)

        def setup_pool(pool):
            pool.memset(minus_half[:], -0.5).then_inc(s_const, 1)
            pool.wait_ge(s_const, 1)
            for step, i in steps:
                if step == "stats":
                    pool.wait_ge(s_cv, i + 1)
                    at_least(pool, s_cz, i)
                    pool.tensor_tensor(rs1[:], var1[:], minus_half[:], ALU.pow).then_inc(s_crs, 1)
                if step == "norm":
                    z = ctx_in[i % 3]
                    if i == 0:
                        pool.wait_ge(s_ln1, 2 * 16)
                    pool.wait_ge(s_cz, i + 1)
                    pool.tensor_tensor(z, z, ln1_w_row, ALU.mult).then_inc(s_czw, 1)
                    pool.wait_ge(s_czw, i + 1)
                    pool.tensor_tensor(z, z, ln1_b_row, ALU.add).then_inc(s_czb, 1)
                if step == "center":
                    n = CENTERED[i]
                    pool.wait_ge(s_wag, 2 * n + 2)
                    rows = stage[i % RING_W].rearrange("p (k d) -> p k d", k=2)
                    means = mv_w[:].rearrange("p (i k s) -> p i k s", i=2, k=2)[:, n % 2, :, 0:1].to_broadcast([P, 2, D])
                    pool.tensor_tensor(rows, rows, means, ALU.subtract).then_inc(s_wc, 1)
                if step == "k0":
                    pool.wait_ge(s_fac, 3)
                    k_prepare_pool(pool, 0)
                    ku_split_lo(pool, 0)
                if step == "x0":
                    pow1(pool, 0)

        def setup_act(act):
            for step, i in steps:
                if step == "split":
                    _, hi, _, col, gate = chunks[i]
                    if i in CENTERED:
                        act.wait_ge(s_wc, CENTERED[i] + 1)
                    else:
                        act.wait_ge(s_stage[i % RING_W], 16 * (i // RING_W + 1))
                    if gate == "w3":
                        act.wait_ge(s_w3[0], 4)
                    if gate == "k":
                        act.wait_ge(s_kv, 24)
                    act.copy(hi[:, col:col + 1024], stage[i % RING_W]).then_inc(s_shi, 1)
                if step in sems_of:
                    made, to_hi, _ = sems_of[step]
                    hi, _, ps = evacuated(step, i)
                    act.wait_ge(made, i + 1)
                    act.copy(hi, ps).then_inc(to_hi, 1)
                if step == "kv":
                    act.wait_ge(s_kv, i + 1)
                    at_least(act, s_kvst[i % 2], 16 * (i // 2))
                    act.copy(kv_out[i % 2], prod_ps[i % 4][:]).then_inc(s_kvo, 1)
                if step == "k0":
                    k_prepare_act(act, 0)

        def setup_dve(dve):
            dve.memset(zero_col[:], 0.0).then_inc(s_ones, 1)
            for half in range(2):
                dve.memset(half_ones[half][:].bitcast(F32), 0.0).then_inc(s_ones, 1)
            dve.memset(bd[:].bitcast(F32), 0.0).then_inc(s_ones, 1)
            dve.wait_ge(s_ones, 4)
            for half in range(2):
                dve.memset(half_ones[half][half * DH:(half + 1) * DH, :].bitcast(F32), 1.0).then_inc(s_ones, 1)
            for step, i in steps:
                if step == "stats":
                    at_least(dve, s_cz, i)
                    dve.wait_ge(s_ctx[i % 3], 16 * (i // 3 + 1))
                    dve.bn_stats(bn1[:], ctx_in[i % 3]).then_inc(s_cbn, 1)
                    dve.wait_ge(s_cbn, i + 1)
                    dve.bn_aggr(mv1[:], bn1[:]).then_inc(s_cag, 1)
                    dve.wait_ge(s_cag, i + 1)
                    dve.tensor_scalar(var1[:], mv1[:, 1:2], EPS, None, ALU.add).then_inc(s_cv, 1)
                if step == "norm":
                    dve.wait_ge(s_crs, i + 1)
                    dve.tensor_scalar(ctx_in[i % 3], ctx_in[i % 3], mv1[:, 0:1], rs1[:, 0:1],
                                      ALU.subtract, ALU.mult).then_inc(s_cz, 1)
                if step == "split":
                    _, hi, lo, col, _ = chunks[i]
                    src = stage[i % RING_W]
                    dve.wait_ge(s_shi, i + 1)
                    dve.tensor_tensor(lo[:, col:col + 1024], src, hi[:, col:col + 1024].bitcast(F32),
                                      ALU.subtract).then_inc(s_slo, 1)
                if step in sems_of:
                    _, to_hi, to_lo = sems_of[step]
                    hi, lo, ps = evacuated(step, i)
                    dve.wait_ge(to_hi, i + 1)
                    dve.tensor_tensor(lo, ps, hi.bitcast(F32), ALU.subtract).then_inc(to_lo, 1)
                if step == "fold":
                    c = WQ_FIRST + i
                    src = stage[c % RING_W]
                    if i == 0:
                        dve.wait_ge(s_rows, 4 * 16)
                        dve.wait_ge(s_turn[0], CTX_TILES)
                    dve.wait_ge(s_stage[c % RING_W], 16 * (c // RING_W + 1))
                    for k in range(2):
                        at_least(dve, s_bq, 2 * i + k)
                        dve.scalar_tensor_tensor(out=ctx_in[2], in0=src[:, k * D:(k + 1) * D], scalar=1.0,
                                                 in1=ln2_b_row, op0=ALU.mult, op1=ALU.mult,
                                                 accum_out=bq[:, 2 * i + k:2 * i + k + 1]).then_inc(s_bq, 1)
                    dve.wait_ge(s_bq, 2 * i + 2)
                    v = src.rearrange("p (k n) -> p k n", k=2)
                    dve.tensor_tensor(v, v, ln2_w_row.unsqueeze(1).to_broadcast([P, 2, D]), ALU.mult).then_inc(s_fold, 1)
                if step == "center":
                    dve.wait_ge(s_stage[i % RING_W], 16 * (i // RING_W + 1))
                    if i >= WQ_FIRST:
                        dve.wait_ge(s_fold, i - WQ_FIRST + 1)
                    at_least(dve, s_wc, CENTERED[i] - 1)
                    for k in range(2):
                        n = 2 * CENTERED[i] + k
                        at_least(dve, s_wag, n)
                        dve.bn_stats(bn_w[:], stage[i % RING_W][:, k * D:(k + 1) * D]).then_inc(s_wbn, 1)
                        dve.wait_ge(s_wbn, n + 1)
                        dve.bn_aggr(mv_w[:, 2 * (n % 4):2 * (n % 4) + 2], bn_w[:]).then_inc(s_wag, 1)
                if step == "factors":
                    dve.tensor_scalar(F_fac[:], fs[:], SCALE, SCALE, ALU.mult, ALU.add).then_inc(s_fac, 1)
                    dve.wait_ge(s_fac, 1)
                    v = lambda a: a[:].rearrange("p (b q) -> p b q", q=PAIRS)
                    dve.tensor_tensor(v(U_fac), v(F_fac), bq[:].unsqueeze(1).to_broadcast([P, B, PAIRS]),
                                      ALU.mult).then_inc(s_fac, 1)
                    dve.wait_ge(s_fac, 2)
                    dve.scalar_tensor_tensor(out=U_fac[:], in0=fs[:], scalar=SCALE, in1=U_fac[:],
                                             op0=ALU.mult, op1=ALU.add).then_inc(s_fac, 1)
                if step == "k0":
                    diag_lo(dve, s_kh, s_kp, 0)
                if step == "x0":
                    ln1_stats(dve, 0, 0)

        def setup_pe(pe):
            for step, i in pe_steps:
                if step == "mix":
                    ks = (2 * i, 2 * i + 1)
                    st = lambda y, k: y[:, k * D + m * P:k * D + (m + 1) * P]
                    mo = lambda y, k: y[:, k * D:(k + 1) * D]
                    pe.wait_ge(s_shi, 2 * i + 2)
                    for m in range(4):
                        for k in ks:
                            pe.matmul(prod_ps[m][:], st(M_hi, k), mo(Wq_hi, k), start=(k == 0), stop=False)
                    pe.wait_ge(s_slo, 2 * i + 2)
                    for m in range(4):
                        for k in ks:
                            pe.matmul(prod_ps[m][:], st(M_hi, k), mo(Wq_lo, k), start=False, stop=False)
                            mm = pe.matmul(prod_ps[m][:], st(M_lo, k), mo(Wq_hi, k), start=False, stop=(k == 3))
                        if i == 1:
                            mm.then_inc(s_a12[0], 1)
                if step == "w3":
                    if i == 0:
                        pe.wait_ge(s_slo, 6)
                        pe.wait_ge(s_a12[2], 4)
                    st = lambda y, k: y[:, 2048 + k * D + i * P:2048 + k * D + (i + 1) * P]
                    mo = lambda y, k: y[:, 2048 + k * D:2048 + (k + 1) * D]
                    passes(pe, prod_ps[i][:], [(st(M_hi, k), st(M_lo, k), mo(Wq_hi, k), mo(Wq_lo, k))
                                               for k in range(DC)]).then_inc(s_w3[0], 1)
                if step == "turn":
                    if i == 0:
                        pe.wait_ge(s_ident, 16)
                    at_least(pe, s_turn[2], i - 3)
                    pe.wait_ge(s_czb, i + 1)
                    for k in range(DC):
                        tr = pe.transpose(turn_bank[i % 4][:, k * P:(k + 1) * P], ctx_in[i % 3][:, k * P:(k + 1) * P], ident[:])
                    tr.then_inc(s_turn[0], 1)
                if step == "kv":
                    which, half, p = kv_where(i)
                    if i == 0:
                        pe.wait_ge(s_slo, WV_FIRST)
                    if i == 8:
                        pe.wait_ge(s_slo, WQ_FIRST)
                    if i in (0, 16):
                        pe.wait_ge(s_turn[2], 4 + 4 * half)
                    if i < 4:
                        pe.wait_ge(s_w3[2], i + 1)
                    else:
                        pe.wait_ge(s_kvo, i - 3)
                    w = (M_hi, M_lo) if which else (Wo_hi, Wo_lo)
                    st = lambda y, k: y[:, k * INNER + p * P:k * INNER + (p + 1) * P]
                    mo = lambda y, k: y[:, k * 1024 + half * BANK:k * 1024 + (half + 1) * BANK]
                    passes(pe, prod_ps[i % 4][:], [(st(w[0], k), st(w[1], k), mo(N_hi, k), mo(N_lo, k))
                                                   for k in range(DC)]).then_inc(s_kv, 1)

        two = lambda name: [sem(f"{name}{i}") for i in range(2)]
        s_xin = [sem(f"s_xin{i}") for i in range(RING)]
        s_xout = [sem(f"s_xout{i}") for i in range(RING)]
        s_kin, s_vin = sem("s_kin"), sem("s_vin")
        s_bn1, s_ag1, s_var1, s_rs1 = (sem(n) for n in ("s_bn1", "s_ag1", "s_var1", "s_rs1"))
        s_bn2, s_ag2, s_var2, s_rs2 = (sem(n) for n in ("s_bn2", "s_ag2", "s_var2", "s_rs2"))
        s_xT = two("s_xT")
        s_xTh, s_xTl = sem("s_xTh"), sem("s_xTl")
        s_x2T, s_x2Th, s_x2Tl = sem("s_x2T"), sem("s_x2Th"), sem("s_x2Tl")
        s_sc, s_sb, s_mx, s_sub, s_ex = two("s_sc"), two("s_sb"), two("s_mx"), two("s_sub"), two("s_ex")
        s_sum, s_inv, s_p = two("s_sum"), two("s_inv"), two("s_p")
        s_pT, s_pTh, s_pTl = two("s_pT"), two("s_pTh"), two("s_pTl")
        s_o, s_x2, s_f, s_fb, s_th, s_y = (sem(n) for n in ("s_o", "s_x2", "s_f", "s_fb", "s_th", "s_y"))
        s_m, s_mh, s_mr, s_mq, s_mlg, s_mlv = (sem(n) for n in ("s_m", "s_mh", "s_mr", "s_mq", "s_mlg", "s_mlv"))
        s_n, s_nh, s_nl = sem("s_n"), sem("s_nh"), sem("s_nl")
        s_bi, s_bs = two("s_bi"), sem("s_bs")
        s_ku, s_ks, s_kuh, s_kh, s_kp = (sem(n) for n in ("s_ku", "s_ks", "s_kuh", "s_kh", "s_kp"))
        s_kul = sem("s_kul")
        s_vh, s_vp = sem("s_vh"), sem("s_vp")

        heads = lambda a: a.rearrange("p (h j) -> p h j", j=CTX)
        half_of = lambda a, q: a[:, q * BANK:(q + 1) * BANK]
        H2 = H // 2

        def diag(part, half):
            blocks = bd[half * DH:(half + 1) * DH, :].rearrange("p (q c) -> p q c", c=2 * P)
            return blocks[:, :, part * P + half * CTX:part * P + (half + 1) * CTX]

        def bd_cols(p, part, n=1):
            return bd[:, (2 * p + part) * P:(2 * p + part + n) * P]

        def dense(y, half):
            return y[half * DH:(half + 1) * DH, :].rearrange("p (q j) -> p q j", j=CTX)

        def of_batch(y, b):
            return y[:, bass.ds(b * PAIRS, PAIRS)].unsqueeze(2).to_broadcast([P, PAIRS, CTX])

        def load_x(sp, u, r):
            at_least(sp, s_xout[r], 4 * (u - r) if not isinstance(u, int) else 16 * (u // RING))
            sp.dma_start(xr[r], x_t[bass.ds(u, 1), :, :].rearrange("o p d -> (o p) d")).then_inc(s_xin[r], 16)

        def load_xT(sp, u, r):
            at_least(sp, s_xTl, u - 1)
            sp.dma_start(xT[r], xT_t[bass.ds(u, 1), :, :].rearrange("o p c -> (o p) c")).then_inc(s_xT[r], 16)

        def x_loaded(eng, u, r):
            eng.wait_ge(s_xin[r], 4 * (u - r) + 16)

        def load_kv(sp, which, b, s):
            src = kv_scratch[which].rearrange("q p b j -> b p q j")[bass.ds(b, 1)].rearrange("o p q j -> (o p) q j")
            sp.dma_start(kvf.rearrange("p (q j) -> p q j", j=CTX), src).then_inc(s, 16)

        def load_k(sp, b):
            at_least(sp, s_vp, b)
            load_kv(sp, 0, b, s_kin)

        def load_v(sp, b):
            sp.wait_ge(s_kp, b + 1)
            load_kv(sp, 1, b, s_vin)

        def k_prepare_pool(pool, b):
            pool.wait_ge(s_kin, 16 * b + 16)
            q = lambda a: a.rearrange("p (q j) -> p q j", j=CTX)
            pool.tensor_tensor(q(kus), q(kvf), of_batch(U_fac, b), ALU.mult).then_inc(s_ku, 1)
            pool.wait_ge(s_ku, b + 1)
            pool.tensor_tensor(q(kvf), q(kvf), of_batch(F_fac, b), ALU.mult).then_inc(s_ks, 1)

        def ku_split_lo(pool, b):
            pool.wait_ge(s_kuh, b + 1)
            pool.tensor_tensor(ku_lo[:], kus, ku_hi[:].bitcast(F32), ALU.subtract).then_inc(s_kul, 1)

        def diag_lo(dve, s_hi, s_done, b):
            dve.wait_ge(s_hi, b + 1)
            for half in range(2):
                last = dve.tensor_tensor(diag(1, half), dense(kvf, half), diag(0, half).bitcast(F32), ALU.subtract)
            last.then_inc(s_done, 1)

        def k_prepare_act(act, b):
            at_least(act, s_bi[1], b)
            act.wait_ge(s_ku, b + 1)
            act.copy(ku_hi[:], kus).then_inc(s_kuh, 1)
            at_least(act, s_n, 8 * b)
            act.wait_ge(s_ks, b + 1)
            for half in range(2):
                last = act.copy(diag(0, half), dense(kvf, half))
            last.then_inc(s_kh, 1)

        def v_prepare_act(act, b):
            act.wait_ge(s_vin, 16 * b + 16)
            act.wait_ge(s_m, 16 * b + 16)
            for half in range(2):
                last = act.copy(diag(0, half), dense(kvf, half))
            last.then_inc(s_vh, 1)

        m_where = lambda c: ((c // 2) % 4, 2 * (c // 8) + c % 2)
        in_pairs = lambda a: a.rearrange("p (i n) -> p i n", i=2)

        def m_ps(c, s):
            return fold_ps[c % 4][:].rearrange("p (i s n) -> p i s n", i=2, s=2)[:, :, s, :]

        def m_part(y, c, dt=F32R):
            dc, g = m_where(c)
            col = dc * INNER + g * 2 * P
            return in_pairs(y[:, col:col + 2 * P].bitcast(dt))

        def m_bank_read(pe, b8, c):
            if c % 2:
                pe.wait_ge(s_mlv, b8 + c // 2 + 1)
            else:
                pe.wait_ge(s_mr, 2 * b8 + c + 1)
                pe.wait_ge(s_mq, b8 + c // 2 + 1)

        def fold_m_pe(pe, b8, cs, free=lambda c: None):
            for c in cs:
                if c == 0:
                    pe.wait_ge(s_kp, b8 // 8 + 1)
                if c < 4:
                    free(c)
                else:
                    m_bank_read(pe, b8, c - 4)
                dc, g = m_where(c)
                for i in range(2):
                    p = 2 * g + i
                    st = lambda y: y[:, p * D + dc * P:p * D + (dc + 1) * P]
                    ps = fold_ps[c % 4][:, i * 2 * P:(i + 1) * 2 * P]
                    pe.matmul(ps, st(Wq_hi), bd_cols(p, 0, 2), start=True, stop=False)
                    mm = pe.matmul(ps[:, 0:P], st(Wq_lo), bd_cols(p, 0), start=False, stop=True)
                mm.then_inc(s_m, 1)

        def bias_pe(pe, b8):
            pe.wait_ge(s_kul, b8 // 8 + 1)
            for half in range(2):
                pe.matmul(bias_ps[half][:], half_ones[half][:], ku_hi[:], start=True, stop=False)
                pe.matmul(bias_ps[half][:], half_ones[half][:], ku_lo[:], start=False, stop=True).then_inc(s_bi[half], 1)

        def m_act(act, b8, cs):
            for c in cs:
                act.wait_ge(s_m, 2 * b8 + c + 1)
                if c % 2 == 0:
                    k = c // 2
                    if k >= 2:
                        act.wait_ge(s_mlg, b8 + k - 1)
                    act.copy(in_pairs(m_cross[k % 2]), m_ps(c, 1)).then_inc(s_mq, 1)
                act.copy(m_part(M_hi, c), m_ps(c, 0)).then_inc(s_mh, 1)

        def m_dve(dve, b8, cs):
            for c in cs:
                k = c // 2
                rest = in_pairs((m_rest_v if c % 2 else m_rest_g)[k % 2])
                if c == 1:
                    dve.wait_ge(s_kul, b8 // 8 + 1)
                if k >= 2:
                    dve.wait_ge(s_mlv if c % 2 else s_mlg, b8 + k - 1)
                dve.wait_ge(s_mh, 2 * b8 + c + 1)
                dve.tensor_tensor(rest, m_ps(c, 0), m_part(M_hi, c, F32), ALU.subtract).then_inc(s_mr, 1)
                if c % 2:
                    dve.wait_ge(s_mr, 2 * b8 + c + 1)
                    dve.tensor_tensor(m_part(M_lo, c), m_ps(c, 1), rest, ALU.add).then_inc(s_mlv, 1)

        def m_pool(pool, b8, ks):
            for k in ks:
                pool.wait_ge(s_mr, 2 * b8 + 2 * k + 1)
                pool.wait_ge(s_mq, b8 + k + 1)
                pool.tensor_tensor(m_part(M_lo, 2 * k), in_pairs(m_rest_g[k % 2]), in_pairs(m_cross[k % 2]),
                                   ALU.add).then_inc(s_mlg, 1)

        def fold_n_pe(pe, b8, ps, free):
            pe.wait_ge(s_vp, b8 // 8 + 1)
            for p in ps:
                if p < 4:
                    free(p)
                else:
                    pe.wait_ge(s_nl, b8 + p - 3)
                mo = lambda y: y[:, p * D:(p + 1) * D]
                passes(pe, fold_ps[p % 4][:], [(bd_cols(p, 0), bd_cols(p, 1), mo(Wo_hi), mo(Wo_lo))]).then_inc(s_n, 1)

        def fold_hi(act, b8, cs, produced, done, dst):
            for c in cs:
                act.wait_ge(produced, b8 + c + 1)
                act.copy(dst(c), fold_ps[c % 4][:]).then_inc(done, 1)

        def fold_lo(dve, b8, cs, produced, done, hi, lo):
            for c in cs:
                dve.wait_ge(produced, b8 + c + 1)
                dve.tensor_tensor(lo(c), fold_ps[c % 4][:], hi(c).bitcast(F32), ALU.subtract).then_inc(done, 1)

        def bias_copy(act, b8):
            for half in range(2):
                act.wait_ge(s_bi[half], b8 // 8 + 1)
                last = act.copy(bias.rearrange("p (q s j) -> p q s j", s=2, j=CTX)[:, :, half, :],
                                       bias_ps[half][:].rearrange("p (q j) -> p q j", j=CTX))
            last.then_inc(s_bs, 1)

        n_cols = lambda y, c: y[:, c * D:(c + 1) * D]
        N_fold = (s_nh, s_nl, lambda c: n_cols(N_hi, c), lambda c: n_cols(N_lo, c))

        def layernorm_stats(dve, src, bn, mv, var, s_bn_, s_ag_, s_var_, s_rs_, u, mul, add, between=None):
            dve.bn_stats(bn[:], src).then_inc(s_bn_, 1)
            dve.wait_ge(s_bn_, u + 1)
            if between:
                between()
            dve.bn_aggr(mv[:], bn[:]).then_inc(s_ag_, 1)
            dve.wait_ge(s_ag_, u + 1)
            at_least(dve, s_rs_, u)
            dve.tensor_scalar(var[:], mv[:, 1:2], mul, add, ALU.mult, ALU.add).then_inc(s_var_, 1)

        def turn(pe, ps, src, s):
            for k in range(4):
                tr = pe.transpose(ps[:, k * P:(k + 1) * P], src[:, k * P:(k + 1) * P], ident[:])
            tr.then_inc(s, 1)

        def ln1_stats(dve, u, r, between=None):
            x_loaded(dve, u, r)
            layernorm_stats(dve, xr[r], bn1, mv1, var1, s_bn1, s_ag1, s_var1, s_rs1, u, 1.0 + EPS,
                            EPS * EPS, between)

        def pow1(pool, u):
            pool.wait_ge(s_var1, u + 1)
            at_least(pool, s_sb[1], u)
            pool.tensor_tensor(rs1[:], var1[:], minus_half[:], ALU.pow).then_inc(s_rs1, 1)

        def xT_split_hi(act, u, r):
            act.wait_ge(s_xT[r], 8 * (u - r) + 16)
            at_least(act, s_sc[1], u)
            act.copy(xT_hi[:], xT[r]).then_inc(s_xTh, 1)

        def xT_split_lo(dve, u, r):
            dve.wait_ge(s_xTh, u + 1)
            at_least(dve, s_sc[1], u)
            dve.tensor_tensor(xT_lo[:], xT[r], xT_hi[:].bitcast(F32), ALU.subtract).then_inc(s_xTl, 1)

        def parts(t, m):
            known = isinstance(t, int)
            return dict(scores=not known or t < T, following=not known or t + 1 < T,
                        attn=not known or 1 <= t <= T, chain=not known or t >= 2,
                        fold_m=m == 7 and (not known or t + 1 < T), fold_n=m == 0 and (not known or t < T),
                        more=not known or t + TPB < T)

        def ended(t, m):
            back = [2]
            if isinstance(t, int):
                back = [] if t < 2 or t == T else [2] if t < T else [3, 2]
            return [(t - k, (m - k) % RING) for k in back]

        def slot_sp(sp, t, m):
            has = parts(t, m)
            fetch = not isinstance(t, int) or t + 2 < T
            if fetch:
                load_xT(sp, t + 2, m % 2)
            if has["more"] and m == 3:
                load_k(sp, (t + 5) // 8)
            if has["more"] and m == 5:
                load_v(sp, (t + 3) // 8)
            if has["chain"]:
                sp.wait_ge(s_y, t - 1)
                r = (m - 2) % RING
                sp.dma_start(out_t[bass.ds(t - 2, 1), :, :].rearrange("o p d -> (o p) d"), xr[r]).then_inc(s_xout[r], 16)
            if fetch:
                load_x(sp, t + 2, (m + 2) % RING)

        def slot_pe(pe, t, m):
            has = parts(t, m)
            first = isinstance(t, int) and t == 0
            attn_first = isinstance(t, int) and t == T
            def turn_x2():
                pe.wait_ge(s_x2, t - 1)
                at_least(pe, s_x2Tl, t - 2)
                turn(pe, x2T_ps, xr[(m - 2) % RING], s_x2T)

            if has["scores"]:
                pe.wait_ge(s_xTh, t + 1)
                for q in range(2):
                    if q == 1 and has["chain"]:
                        turn_x2()
                    if m == 0:
                        pe.wait_ge(s_mlg, t + 4 * q + 4)
                        pe.wait_ge(s_mlv, t + 4 * q + 4)
                        m_bank_read(pe, t, 12 + q)
                    if m == 1:
                        pe.wait_ge(s_nl, t + 4 + q)
                    at_least(pe, s_sb[q], t)
                    mo = lambda y, k: y[:, k * INNER + q * BANK:k * INNER + (q + 1) * BANK]
                    st = lambda y, k: y[:, k * P:(k + 1) * P]
                    passes(pe, S_ps[q][:], [(st(xT_hi, k), st(xT_lo, k), mo(M_hi, k), mo(M_lo, k)) for k in range(DC)],
                           (lambda: pe.wait_ge(s_xTl, t + 1)) if q == 0 else None).then_inc(s_sc[q], 1)

            def chain():
                pe.wait_ge(s_x2Th, t - 1)
                at_least(pe, s_fb, t - 2)
                st = lambda y, k: y[:, k * P:(k + 1) * P]
                mo = lambda y, k: y[:, k * D:(k + 1) * D]

                def before_lo():
                    if has["fold_m"]:
                        fold_m_pe(pe, t + 1, (0, 1), lambda c: pe.wait_ge(s_sb[c], t + 1))
                    pe.wait_ge(s_x2Tl, t - 1)
                passes(pe, F_ps[:], [(st(x2T_hi, k), st(x2T_lo, k), mo(W3_hi, k), mo(W3_lo, k)) for k in range(DC)],
                       before_lo).then_inc(s_f, 1)

            if has["chain"] and not has["scores"] and not attn_first:
                turn_x2()
            if has["fold_m"]:
                pe.wait_ge(s_x2, t - 1)
                bias_pe(pe, t + 1)
            if has["attn"]:
                if m == 1:
                    pe.wait_ge(s_nl, t + 7)
                for q in range(2):
                    pe.wait_ge(s_p[q], t)
                    at_least(pe, s_pTl[q], t - 1)
                    turn(pe, pT_ps[q], half_of(S[(m - 1) % 2], q), s_pT[q])
            if has["chain"] and not attn_first:
                chain()
            if has["attn"]:
                at_least(pe, s_x2, t - 1)
            if first:
                fold_n_pe(pe, t, range(4), lambda c: pe.wait_ge(s_sb[c], t + 1) if c < 2 else None)
            for quarter in range(4):
                if has["fold_m"]:
                    fold_m_pe(pe, t + 1, ((2, 3, 4), (5, 6, 7), (8, 9, 10, 11), (12, 13, 14, 15))[quarter],
                              lambda c: pe.wait_ge(s_pTl[c - 2], t))
                    if quarter == 0:
                        pe.wait_ge(s_bs, (t + 1) // 8 + 1)
                if has["attn"]:
                    q, ks = quarter // 2, (2 * quarter, 2 * quarter + 1)
                    pe.wait_ge(s_pTh[q], t)
                    for k in ks:
                        for mv in (N_hi, N_lo):
                            pe.matmul(O_ps[:], pT_hi[:, k * P:(k + 1) * P], n_cols(mv, k),
                                      start=(k == 0 and mv is N_hi), stop=False)
                    pe.wait_ge(s_pTl[q], t)
                    for k in ks:
                        mm = pe.matmul(O_ps[:], pT_lo[:, k * P:(k + 1) * P], n_cols(N_hi, k), start=False, stop=(k == 7))
                    if quarter == 3:
                        mm.then_inc(s_o, 1)
            if has["fold_n"]:
                fold_n_pe(pe, t, range(4 * first, 8), lambda c: pe.wait_ge(s_sb[c], t + 1) if c < 2 else None)
            if has["chain"] and attn_first:
                turn_x2()
                chain()

        def slot_act(act, t, m):
            has = parts(t, m)
            first = isinstance(t, int) and t == 0
            attn_first = isinstance(t, int) and t == T

            def exp(q):
                act.wait_ge(s_sub[q], t + 1)
                s = half_of(S[m % 2], q)
                act.activation(s, s, ACT.Exp).then_inc(s_ex[q], 1)

            def x2T_hi_part():
                act.wait_ge(s_x2T, t - 1)
                at_least(act, s_f, t - 2)
                act.copy(x2T_hi[:], x2T_ps[:]).then_inc(s_x2Th, 1)

            if has["chain"] and not attn_first:
                x2T_hi_part()
            if has["attn"]:
                at_least(act, s_o, t - 1)
                for q in range(2):
                    act.wait_ge(s_pT[q], t)
                    act.copy(half_of(pT_hi, q), pT_ps[q][:]).then_inc(s_pTh[q], 1)
            if has["chain"] and attn_first:
                x2T_hi_part()
            if has["scores"]:
                exp(0)
                if has["following"]:
                    xT_split_hi(act, t + 1, (m + 1) % 2)
                if first:
                    fold_hi(act, t, range(6), s_n, s_nh, N_fold[2])
                exp(1)
            if has["fold_n"] and not first:
                v_prepare_act(act, t // 8)
            if has["more"] and m == 4:
                k_prepare_act(act, (t + 4) // 8)
            if has["fold_m"]:
                m_act(act, t + 1, range(2))
                bias_copy(act, t + 1)
                m_act(act, t + 1, range(2, 10))
            for u, _ in ended(t, m):
                act.wait_ge(s_fb, u + 1)
                act.activation(hid, hid, ACT.Tanh).then_inc(s_th, 1)
            if has["fold_m"]:
                m_act(act, t + 1, range(10, 16))
            if has["fold_n"]:
                fold_hi(act, t, range(6 * first, 8), s_n, s_nh, N_fold[2])

        def slot_dve(dve, t, m):
            has = parts(t, m)
            first = isinstance(t, int) and t == 0
            r2 = (m - 2) % RING

            attn_first = isinstance(t, int) and t == T

            def x2T_lo_part():
                dve.wait_ge(s_x2Th, t - 1)
                at_least(dve, s_f, t - 2)
                dve.tensor_tensor(x2T_lo[:], x2T_ps[:], x2T_hi[:].bitcast(F32), ALU.subtract).then_inc(s_x2Tl, 1)

            def pT_lo_part():
                at_least(dve, s_o, t - 1)
                for q in range(2):
                    dve.wait_ge(s_pTh[q], t)
                    dve.tensor_tensor(half_of(pT_lo, q), pT_ps[q][:], half_of(pT_hi, q).bitcast(F32),
                                      ALU.subtract).then_inc(s_pTl[q], 1)

            def add_bias(u):
                dve.wait_ge(s_f, u + 1)
                at_least(dve, s_y, u)
                dve.wait_ge(s_rs2, u + 1)
                dve.scalar_tensor_tensor(out=hid, in0=F_ps[:], scalar=rs2[:, 0:1], in1=ffn_bias_row[:],
                                         op0=ALU.mult, op1=ALU.add).then_inc(s_fb, 1)

            def read_scores(q):
                dve.wait_ge(s_sc[q], t + 1)
                at_least(dve, s_pT[q], t - 1)
                if m == 0 and q == 0:
                    dve.wait_ge(s_bs, t // 8 + 1)
                    dve.wait_ge(s_mlg, t + 8)
                dve.wait_ge(s_rs1, t + 1)
                dve.scalar_tensor_tensor(out=half_of(S[m % 2], q), in0=S_ps[q][:], scalar=rs1[:, 0:1],
                                         in1=half_of(bias, q), op0=ALU.mult, op1=ALU.add).then_inc(s_sb[q], 1)

            def maximum(q):
                dve.wait_ge(s_sb[q], t + 1)
                dve.tensor_reduce(row_max[m % 2][:, q * H2:(q + 1) * H2], heads(half_of(S[m % 2], q)), AX_X,
                                  ALU.max).then_inc(s_mx[q], 1)

            if has["chain"]:
                dve.wait_ge(s_o, t - 1)
                dve.tensor_tensor(xr[r2], O_ps[:], xr[r2], ALU.add).then_inc(s_x2, 1)
                if attn_first:
                    pT_lo_part()
                dve.wait_ge(s_x2, t - 1)
                layernorm_stats(dve, xr[r2], bn2, mv2, var2, s_bn2, s_ag2, s_var2, s_rs2, t - 2, 1.0, EPS,
                                (lambda: read_scores(0)) if has["scores"] else None)
            elif has["scores"]:
                read_scores(0)
            if has["scores"]:
                maximum(0)
            if has["scores"]:
                read_scores(1)
            for u, _ in ended(t, m)[:-1]:
                add_bias(u)
            if has["chain"] and not attn_first:
                x2T_lo_part()
            if first:
                fold_lo(dve, t, range(2), *N_fold)
            if has["scores"]:
                maximum(1)
            if has["fold_m"]:
                ln1_stats(dve, t + 1, (m + 1) % RING, pT_lo_part)
            elif has["attn"] and not attn_first:
                pT_lo_part()
            if has["chain"] and attn_first:
                x2T_lo_part()
            if has["following"] and not has["fold_m"] and not first:
                ln1_stats(dve, t + 1, (m + 1) % RING, lambda: xT_split_lo(dve, t + 1, (m + 1) % 2))
            if has["fold_n"] and not first:
                diag_lo(dve, s_vh, s_vp, t // 8)
            if has["fold_n"] and first:
                fold_lo(dve, t, range(2, 4), *N_fold)
                xT_split_lo(dve, 1, 1)
                fold_lo(dve, t, range(4, 8), *N_fold)
                ln1_stats(dve, 1, 1)
            if has["fold_m"]:
                m_dve(dve, t + 1, range(2))
            if has["scores"]:
                for q in range(2):
                    hs = slice(q * H2, (q + 1) * H2)
                    dve.wait_ge(s_ex[q], t + 1)
                    dve.tensor_reduce(row_sum[m % 2][:, hs], heads(half_of(S[m % 2], q)), AX_X, ALU.add).then_inc(s_sum[q], 1)
                    if has["fold_m"]:
                        m_dve(dve, t + 1, range(2 + 2 * q, 4 + 2 * q))
                    dve.wait_ge(s_sum[q], t + 1)
                    dve.reciprocal(row_inv[m % 2][:, hs], row_sum[m % 2][:, hs]).then_inc(s_inv[q], 1)
            for u, _ in ended(t, m)[-1:]:
                add_bias(u)
            if has["more"] and m == 4:
                diag_lo(dve, s_kh, s_kp, (t + 4) // 8)
            if has["fold_m"]:
                m_dve(dve, t + 1, range(6, 12))
                xT_split_lo(dve, t + 1, (m + 1) % 2)
                m_dve(dve, t + 1, range(12, 16))
            if has["fold_n"] and not first:
                fold_lo(dve, t, range(8), *N_fold)

        def slot_pool(pool, t, m):
            has = parts(t, m)

            def by_head(q, row, op, s_wait, s_done):
                s = heads(half_of(S[m % 2], q))
                pool.wait_ge(s_wait[q], t + 1)
                pool.tensor_tensor(s, s, row[m % 2][:, q * H2:(q + 1) * H2].unsqueeze(2).to_broadcast([P, H2, CTX]),
                                   op).then_inc(s_done[q], 1)

            if has["chain"]:
                pool.wait_ge(s_var2, t - 1)
                at_least(pool, s_fb, t - 2)
                pool.tensor_tensor(rs2[:], var2[:], minus_half[:], ALU.pow).then_inc(s_rs2, 1)
            if has["scores"]:
                by_head(0, row_max, ALU.subtract, s_mx, s_sub)
            if has["scores"]:
                by_head(1, row_max, ALU.subtract, s_mx, s_sub)
            if has["following"]:
                pow1(pool, t + 1)
            if has["fold_m"]:
                m_pool(pool, t + 1, range(1))
            if has["scores"]:
                by_head(0, row_inv, ALU.mult, s_inv, s_p)
            if has["fold_m"]:
                m_pool(pool, t + 1, range(1, 3))
            if has["scores"]:
                by_head(1, row_inv, ALU.mult, s_inv, s_p)
            if has["fold_m"]:
                m_pool(pool, t + 1, range(3, 5))
            for u, r2 in ended(t, m):
                pool.wait_ge(s_th, u + 1)
                pool.tensor_tensor(xr[r2], xr[r2], hid, ALU.add).then_inc(s_y, 1)
            if has["fold_m"]:
                m_pool(pool, t + 1, range(5, 8))
            if has["more"] and m == 3:
                k_prepare_pool(pool, (t + 5) // 8)
            if has["more"] and m == 4:
                ku_split_lo(pool, (t + 4) // 8)

        def run(eng, slot):
            for t in range(3):
                slot(eng, t, t)
            with eng.Fori(0, B - 1) as b:
                for j in range(3, TPB + 3):
                    slot(eng, b * TPB + j, j % TPB)
            for t in range(T - 5, T + 2):
                slot(eng, t, t % TPB)

        with nc.Block() as block:
            @block.sync
            def _(sp):
                setup_sp(sp)
                run(sp, slot_sp)
                for r in range(RING):
                    sp.wait_ge(s_xout[r], 16 * (T // RING))

            @block.tensor
            def _(pe):
                setup_pe(pe)
                pe.wait_ge(s_slo, CHUNKS)
                fold_m_pe(pe, 0, range(16))
                pe.wait_ge(s_kvo, 4 * PAIRS)
                bias_pe(pe, 0)
                run(pe, slot_pe)

            @block.scalar
            def _(act):
                setup_act(act)
                m_act(act, 0, range(8))
                xT_split_hi(act, 0, 0)
                m_act(act, 0, range(8, 16))
                bias_copy(act, 0)
                v_prepare_act(act, 0)
                run(act, slot_act)

            @block.vector
            def _(dve):
                setup_dve(dve)
                m_dve(dve, 0, range(16))
                xT_split_lo(dve, 0, 0)
                diag_lo(dve, s_vh, s_vp, 0)
                run(dve, slot_dve)

            @block.gpsimd
            def _(pool):
                setup_pool(pool)
                m_pool(pool, 0, range(8))
                run(pool, slot_pool)


def kernel(x, ctx_1024, fside_Bx16_0, L0_xattn_ln1_w, L0_xattn_ln1_b, L0_xattn_ln2_w, L0_xattn_ln2_b,
           L0_xattn_Wq, L0_xattn_Wkv, L0_xattn_Wout, L0_ffn_weight, L0_ffn_aux_weight1, L0_ffn_aux_weight2,
           L0_ffn_bias):
    import concourse.bacc as bacc
    from concourse.bass_utils import run_bass_kernel_spmd

    fs_cols = np.ascontiguousarray(
        np.repeat(np.asarray(fside_Bx16_0).reshape(B, PAIRS, 2).transpose(2, 0, 1).reshape(2, 1, B * PAIRS), P // 2, axis=1)
        .reshape(P, B * PAIRS))
    arrays = {
        "x": np.ascontiguousarray(x),
        "x_turned": np.ascontiguousarray(np.asarray(x).reshape(T, P, DC, P).transpose(0, 3, 2, 1).reshape(T, P, D)),
        "ctx_rows": np.ascontiguousarray(np.asarray(ctx_1024).reshape(B * CTX, D)),
        "fs_cols": fs_cols,
        "ln1_w": np.ascontiguousarray(L0_xattn_ln1_w), "ln1_b": np.ascontiguousarray(L0_xattn_ln1_b),
        "ln2_w": np.ascontiguousarray(L0_xattn_ln2_w), "ln2_b": np.ascontiguousarray(L0_xattn_ln2_b),
        "wqT": np.ascontiguousarray(np.asarray(L0_xattn_Wq).T),
        "wkv": np.ascontiguousarray(L0_xattn_Wkv), "wout": np.ascontiguousarray(L0_xattn_Wout),
        "ffn_wT": np.ascontiguousarray(np.asarray(L0_ffn_weight).T),
        "aux1T": np.ascontiguousarray(np.asarray(L0_ffn_aux_weight1).T),
        "aux2": np.ascontiguousarray(L0_ffn_aux_weight2),
        "ffn_bias": np.ascontiguousarray(L0_ffn_bias),
        "ident_in": np.eye(P, dtype=np.float32),
    }
    nc = bacc.Bacc("TRN2", target_bir_lowering=False, num_devices=1)
    args = [nc.dram_tensor(f"{name}_dram", a.shape, mybir.dt.from_np(a.dtype), kind="ExternalInput").ap()
            for name, a in arrays.items()]
    out = nc.dram_tensor("y_dram", (B, ROWS, D), F32, kind="ExternalOutput").ap()
    build(nc, *args, out)
    r = run_bass_kernel_spmd(nc, [{f"{name}_dram": a for name, a in arrays.items()}], core_ids=[0])
    return r.results[0]["y_dram"]
```
